# Optimizing a Trainium2 kernel written in Bass

```python
import numpy as np
import jax
import jax.numpy as jnp

def _softmax(x, axis=-1):
    return jax.nn.softmax(x, axis=axis)

def _gelu(x):
    return jax.nn.gelu(x, approximate=True)

def _silu(x):
    return jax.nn.silu(x)

def _sigmoid(x):
    return jax.nn.sigmoid(x)

def _layernorm(x, axis=-1, eps=1e-05):
    m = jnp.mean(x, axis=axis, keepdims=True)
    v = jnp.var(x, axis=axis, keepdims=True)
    return (x - m) / jnp.sqrt(v + eps)

def _scatter_add(tgt, idx, src, axis=0):
    return tgt.at[idx].add(src)

def _segment_sum(src, seg, n):
    return jax.ops.segment_sum(src, seg, n)
kernel_name = 'mk_lm_tower_d1_tok_ids768_r4_418d0b'

def setup_inputs(seed: int=0):
    np.random.seed(seed)
    _w = jnp.asarray

    def _rec_inputs():
        import jax
        import jax.numpy as jnp
        _rk = jax.random.key(seed)
        x = jax.random.randint(jax.random.fold_in(_rk, 1), (16, 256), 0, 127999, jnp.int32)
        return x
    x = _rec_inputs()

    def _L0_tok_setup():
        import jax, jax.numpy as jnp
        import numpy as np
        import math
        VOCAB = 32000
        BASIN_DIM = 64
        D_MODEL = 192
        EPS = 1e-08
        key = jax.random.key(seed)
        k1, k2, k3, k4 = jax.random.split(key, 4)
        token_ids = jax.random.randint(k1, (8, 1024), 0, VOCAB, dtype=jnp.int32)
        coords = jax.random.normal(k2, (VOCAB, BASIN_DIM), dtype=jnp.float32)
        coords = coords / jnp.linalg.norm(coords, axis=-1, keepdims=True)
        coords = coords * (math.sqrt(BASIN_DIM) / 5.0)
        coords = coords + jax.random.normal(k3, coords.shape, dtype=jnp.float32) * 0.01
        w = jax.random.normal(k4, (D_MODEL, BASIN_DIM), dtype=jnp.float32)
        q, _ = jnp.linalg.qr(w)
        proj_w = q * 0.1
        norm_w = jnp.ones((D_MODEL,), dtype=jnp.float32)
        return {'token_ids': token_ids, 'basin_coords': coords, 'proj_w': proj_w, 'norm_w': norm_w}
    _L0_tok_all = _L0_tok_setup()
    _L0_tok_in = {k: v for k, v in _L0_tok_all.items() if k in ('basin_coords', 'proj_w', 'norm_w')}
    del _L0_tok_all

    def _L0_attn_setup():
        import jax, jax.numpy as jnp
        import numpy as np
        D = 192
        key = jax.random.key(seed)
        ks = jax.random.split(key, 9)
        B, S = (4, 1024)
        s = 0.02
        return {'x': jax.random.normal(ks[0], (B, S, D), dtype=jnp.float32), 'Wq': jax.random.normal(ks[1], (D, D), dtype=jnp.float32) * s, 'bq': jax.random.normal(ks[2], (D,), dtype=jnp.float32) * s, 'Wk': jax.random.normal(ks[3], (D, D), dtype=jnp.float32) * s, 'bk': jax.random.normal(ks[4], (D,), dtype=jnp.float32) * s, 'Wv': jax.random.normal(ks[5], (D, D), dtype=jnp.float32) * s, 'bv': jax.random.normal(ks[6], (D,), dtype=jnp.float32) * s, 'Wc': jax.random.normal(ks[7], (D, D), dtype=jnp.float32) * s, 'bc': jax.random.normal(ks[8], (D,), dtype=jnp.float32) * s}
    _L0_attn_all = _L0_attn_setup()
    _L0_attn_in = {k: v for k, v in _L0_attn_all.items() if k in ('Wq', 'bq', 'Wk', 'bk', 'Wv', 'bv', 'Wc', 'bc')}
    del _L0_attn_all

    def _L0_ffn_setup():
        import jax, jax.numpy as jnp
        import numpy as np
        B, T, C = (4, 512, 192)
        E, K = (8, 2)

        def _mlp(x, wfc, wproj):
            h = jnp.square(jax.nn.relu(x @ wfc))
            return h @ wproj
        key = jax.random.key(seed)
        ks = jax.random.split(key, 6)
        s = 0.02
        return {'x': jax.random.normal(ks[0], (B, T, C), jnp.float32), 'w_fc_sh': jax.random.normal(ks[1], (C, C), jnp.float32) * s, 'w_proj_sh': jax.random.normal(ks[2], (C, C), jnp.float32) * s, 'w1': jax.random.normal(ks[3], (E, C, C), jnp.float32) * s, 'w2': jax.random.normal(ks[4], (E, C, C), jnp.float32) * s, 'router_w': jax.random.normal(ks[5], (E, C), jnp.float32) * s, 'balance_bias': jnp.zeros((E,), jnp.float32)}
    _L0_ffn_all = _L0_ffn_setup()
    _L0_ffn_in = {k: v for k, v in _L0_ffn_all.items() if k in ('w_fc_sh', 'w_proj_sh', 'w1', 'w2', 'router_w', 'balance_bias')}
    del _L0_ffn_all
    return {'x': x, 'L0_tok_basin_coords': _L0_tok_in['basin_coords'], 'L0_tok_proj_w': _L0_tok_in['proj_w'], 'L0_tok_norm_w': _L0_tok_in['norm_w'], 'L0_attn_Wq': _L0_attn_in['Wq'], 'L0_attn_bq': _L0_attn_in['bq'], 'L0_attn_Wk': _L0_attn_in['Wk'], 'L0_attn_bk': _L0_attn_in['bk'], 'L0_attn_Wv': _L0_attn_in['Wv'], 'L0_attn_bv': _L0_attn_in['bv'], 'L0_attn_Wc': _L0_attn_in['Wc'], 'L0_attn_bc': _L0_attn_in['bc'], 'L0_ffn_w_fc_sh': _L0_ffn_in['w_fc_sh'], 'L0_ffn_w_proj_sh': _L0_ffn_in['w_proj_sh'], 'L0_ffn_w1': _L0_ffn_in['w1'], 'L0_ffn_w2': _L0_ffn_in['w2'], 'L0_ffn_router_w': _L0_ffn_in['router_w'], 'L0_ffn_balance_bias': _L0_ffn_in['balance_bias']}

def reference(x, L0_tok_basin_coords, L0_tok_proj_w, L0_tok_norm_w, L0_attn_Wq, L0_attn_bq, L0_attn_Wk, L0_attn_bk, L0_attn_Wv, L0_attn_bv, L0_attn_Wc, L0_attn_bc, L0_ffn_w_fc_sh, L0_ffn_w_proj_sh, L0_ffn_w1, L0_ffn_w2, L0_ffn_router_w, L0_ffn_balance_bias):
    import jax
    import jax.numpy as jnp

    def _L0_tok_ref(token_ids, basin_coords, proj_w, norm_w):
        import jax, jax.numpy as jnp
        import numpy as np
        import math
        VOCAB = 32000
        BASIN_DIM = 64
        D_MODEL = 192
        EPS = 1e-08
        basin = basin_coords[token_ids]
        emb = jnp.einsum('bsk,dk->bsd', basin, proj_w)
        x_f = emb.astype(jnp.float32)
        rms = jnp.sqrt(jnp.mean(x_f * x_f, axis=-1, keepdims=True) + EPS)
        y = (x_f / rms).astype(emb.dtype)
        return y * norm_w

    def _L0_attn_ref(x, Wq, bq, Wk, bk, Wv, bv, Wc, bc):
        import jax, jax.numpy as jnp
        import numpy as np
        D = 192
        B, S, nd = x.shape
        q = jnp.einsum('bsd,ed->bse', x, Wq) + bq
        k = jnp.einsum('bsd,ed->bse', x, Wk) + bk
        v = jnp.einsum('bsd,ed->bse', x, Wv) + bv
        att = jnp.einsum('bqd,bkd->bqk', q, k) * nd ** (-0.5)
        att = jax.nn.softmax(att, axis=-1)
        y = jnp.einsum('bqk,bkd->bqd', att, v)
        y = jnp.transpose(y, (0, 2, 1)).reshape(B, S, nd)
        return jnp.einsum('bsd,ed->bse', y, Wc) + bc

    def _L0_ffn_ref(x, w_fc_sh, w_proj_sh, w1, w2, router_w, balance_bias):
        import jax, jax.numpy as jnp
        import numpy as np
        B, T, C = (4, 512, 192)
        E, K = (8, 2)

        def _mlp(x, wfc, wproj):
            h = jnp.square(jax.nn.relu(x @ wfc))
            return h @ wproj
        Bx, Tx, Cx = x.shape
        shared = _mlp(x, w_fc_sh, w_proj_sh)
        xf = x.reshape(-1, Cx)
        logits = xf.astype(jnp.float32) @ router_w.T
        scores = jax.nn.sigmoid(logits)
        _, idx = jax.lax.top_k(scores + balance_bias, K)
        tw = jnp.take_along_axis(scores, idx, axis=-1)
        tw = tw / (tw.sum(-1, keepdims=True) + 1e-20)
        combine = (jax.nn.one_hot(idx, E, dtype=tw.dtype) * tw[..., None]).sum(1)
        h = jnp.square(jax.nn.relu(jnp.einsum('nc,ech->neh', xf, w1)))
        y = jnp.einsum('neh,ehc->nec', h, w2)
        routed = jnp.einsum('nec,ne->nc', y, combine)
        return shared + routed.reshape(Bx, Tx, Cx)
    h = _L0_tok_ref(x, L0_tok_basin_coords, L0_tok_proj_w, L0_tok_norm_w)
    h = h + _L0_attn_ref(_layernorm(h, axis=-1), L0_attn_Wq, L0_attn_bq, L0_attn_Wk, L0_attn_bk, L0_attn_Wv, L0_attn_bv, L0_attn_Wc, L0_attn_bc)
    h = h + _L0_ffn_ref(_layernorm(h, axis=-1), L0_ffn_w_fc_sh, L0_ffn_w_proj_sh, L0_ffn_w1, L0_ffn_w2, L0_ffn_router_w, L0_ffn_balance_bias)
    return h

_drawn_inputs = setup_inputs


def setup_inputs(seed=0):
    import zlib

    import numpy as np

    out = dict(_drawn_inputs(seed))
    spreads = {'L0_tok_norm_w': (1.0, 0.2), 'L0_ffn_balance_bias': (0.0, 0.515)}
    factors = {'L0_attn_Wq': 8.0,
     'L0_attn_bq': 8.0,
     'L0_attn_Wk': 8.0,
     'L0_attn_bk': 8.0,
     'L0_attn_bv': 8.0,
     'L0_attn_bc': 2.841,
     'L0_ffn_w_fc_sh': 2.748,
     'L0_ffn_w1': 3.751,
     'L0_ffn_w2': 3.346,
     'L0_ffn_router_w': 3.7}
    for name, (base, spread) in spreads.items():
        noise = np.random.default_rng([zlib.crc32(name.encode()), seed]).standard_normal(out[name].shape)
        drawn = base * np.exp(spread * noise) if base else spread * noise
        out[name] = jnp.asarray(drawn.astype(out[name].dtype))
    for name, factor in factors.items():
        out[name] = (out[name] * factor).astype(out[name].dtype)
    return out
```

```python
import concourse.bass as bass
from concourse import mybir
from contextlib import ExitStack

P = 128
D = 192
KD = 64
DR = D - P
VOCAB = 32000
BATCH, SEQ = 16, 256
GT = 512
STEPS = BATCH * SEQ // GT
TR = GT // P
SG = GT // SEQ
QT = SEQ // P
NE = 8
HID = (NE + 1) * D
NCH = -(-HID // P)
ECH = NE * D // P
HP = NCH * P
LAG = 3
SCALE = float(D) ** -0.5
EPS_RMS, EPS_LN, EPS_TOP = 1e-8, 1e-5, 1e-20
BIG = 3.0e38


class Group:

    def __init__(self, i, off):
        self.n = 2 * i + off if off else 2 * i
        self.par = off % 2
        self.half = i + off // 2 if off // 2 else i

    def of(self, each, k):
        return self.n * each + k if k else self.n * each


def tower_kernel(nc, x, coords, w_proj, norm_w, w_qk, b_qk, w_v, b_v, w_c, b_c, w_up, w_down, w_router, b_bal, out):
    f32, f32r, i32 = mybir.dt.float32, mybir.dt.float32r, mybir.dt.int32
    ALU, ACT, AX = mybir.AluOpType, mybir.ActivationFunctionType, mybir.AxisListType

    ids_v = x.rearrange("b s -> (b s)").rearrange("(n p r) -> p n r", p=P, r=TR)
    out_v = out.rearrange("b s d -> (b s d)").rearrange("(n p f) -> n p f", p=P, f=TR * D)
    comb_dram = nc.dram_tensor("comb_scratch", (2, NE, GT), f32).ap()

    ctx = ExitStack()
    with ctx:
        def sb(name, shape, dt=f32):
            return ctx.enter_context(nc.sbuf_tensor(name, shape, dt))

        def sem(name):
            return ctx.enter_context(nc.semaphore(name))

        ident = sb("ident", [P, P])
        ones = sb("ones", [P, P], f32r)
        nhalf = sb("nhalf", [P, TR])
        rank = sb("rank", [P, TR, NE])
        normw = sb("normw", [P, D])
        balb = sb("balb", [P, NE])
        bqk = sb("bqk", [P, 3])
        PJh, PJl = sb("PJh", [P, D], f32r), sb("PJl", [P, D], f32r)
        QK0h, QK0l, QK1h, QK1l = [sb(f"QK{s}", [P, 2 * D], f32r) for s in ("0h", "0l", "1h", "1l")]
        WV0h, WV0l, WV1h, WV1l = [sb(f"WV{s}", [P, D], f32r) for s in ("0h", "0l", "1h", "1l")]
        WCh, WCl = [sb(f"WC{s}", [P, 4, D], f32r) for s in ("h", "l")]
        RW0h, RW0l, RW1h, RW1l = [sb(f"RW{s}", [P, NE], f32r) for s in ("0h", "0l", "1h", "1l")]
        BVC = sb("BVC", [P, 2 * D], f32r)
        UP0h, UP0l, UP1h, UP1l = [sb(f"UP{s}", [P, HP], f32r) for s in ("0h", "0l", "1h", "1l")]
        DNh, DNl = [sb(f"DN{s}", [P, NCH, D], f32r) for s in ("h", "l")]
        ids = sb("ids", [P, STEPS, TR], i32)
        rows = sb("rows", [P, STEPS, TR], i32)
        row_now = [sb(f"row_now{i}", [P, TR], i32) for i in range(2)]
        G = [sb(f"G{i}", [P, TR, KD]) for i in range(2)]
        GTs = sb("GTs", [P, GT], f32r)
        ss = sb("ss", [P, TR])
        Fw = sb("Fw", [P, TR, D])
        st = sb("st", [P, TR, 6])
        idf, neg = [Fw[:, i, 0:STEPS * TR].rearrange("p (n r) -> p n r", r=TR) for i in range(2)]
        mm = sb("mm", [P, 6, TR])
        sA = sb("sA", [P, 4, TR])
        sr1 = sb("sr1", [P, TR])
        sscl = sb("sscl", [P, TR])
        h = sb("h", [P, TR, D])
        xn = sb("xn", [P, 2, 2 * D])
        X0h, X0l, X1 = [sb(f"X{s}", [P, GT], f32r) for s in ("0h", "0l", "1")]
        QB, KB = sb("QB", [P, 2, GT], f32r), sb("KB", [P, 2, GT], f32r)
        Q0h, Q0l, K0h, K0l = QB[:, 0, :], QB[:, 1, :], KB[:, 0, :], KB[:, 1, :]
        Q1 = sb("Q1", [P, GT], f32r)
        K1h, K1l = sb("K1h", [P, GT], f32r), sb("K1l", [P, GT], f32r)
        Vh, Vl = [sb(f"V{s}", [P, TR, D], f32r) for s in ("h", "l")]
        mx = sb("mx", [P, SG, QT])
        nb = sb("nb", [P, SG, QT])
        rs = sb("rs", [P, SG, QT])
        ri = sb("ri", [P, SG, QT])
        Pr = sb("Pr", [P, SG, QT, SEQ])
        PTh, PTl = [sb(f"PT{s}", [P, SG, QT, SEQ], f32r) for s in ("h", "l")]
        Yh, Yl = [t[:, :, :].rearrange("p a b -> p (a b)")[:, 0:TR * D]
                  .rearrange("p (q c s a) -> p q c s a", q=QT, c=3, s=SG) for t in (QB, KB)]
        h2 = [sb(f"h2{i}", [P, TR, D]) for i in range(2)]
        st2 = sb("st2", [P, TR, 6])
        mm2 = sb("mm2", [P, 6, TR])
        ve2 = sb("ve2", [P, TR])
        s2 = sb("s2", [P, TR])
        Z0h, Z0l, Z1 = [[sb(f"Z{s}_{i}", [P, GT], f32r) for i in range(2)] for s in ("0h", "0l", "1")]
        rt = sb("rt", [P, 14, TR, NE])
        rm = sb("rm", [P, 6, TR])
        combT = sb("combT", [P, P])
        combB = [sb(f"combB{i}", [P, ECH, GT]) for i in range(2)]
        R = [sb(f"R{i}", [P, GT]) for i in range(2)]
        U = [sb(f"U{i}", [P, GT]) for i in range(2)]
        Uh, Ul = [[sb(f"U{s}{i}", [P, GT], f32r) for i in range(2)] for s in ("h", "l")]
        raw0 = combB[0][:, :, :].rearrange("p a b -> p (a b)")
        raw1 = combB[1][:, :, :].rearrange("p a b -> p (a b)")
        at = [0]

        def raw(base, n):
            at[0] += n
            assert at[0] <= ECH * GT
            return base[:, at[0] - n:at[0]]
        rPJ = raw(raw0, D)
        rQK0, rQK1 = raw(raw0, 2 * D), raw(raw0, 2 * D)
        rWV0, rWV1 = raw(raw0, D), raw(raw0, D)
        rWC = raw(raw0, 4 * D)
        rRW0, rRW1 = raw(raw0, NE), raw(raw0, NE)
        rB = raw(raw0, 2 * D)
        rDN = raw(raw0, NCH * D)
        at[0] = 0
        rUP0, rUP1 = raw(raw1, HP), raw(raw1, HP)

        def bank(name):
            return ctx.enter_context(nc.psum_tensor(name, [P, 512], f32))
        A = [bank("A0"), bank("A1")]
        B = [bank("B0"), bank("B1")]
        UB = [bank("U0p"), bank("U1p")]
        AC = [bank("acc0"), bank("acc1")]

        def two(t):
            return t[:, 0:2 * D].rearrange("p (a d) -> p a d", a=2)

        def halves(t):
            return t[:, 0:2 * P].rearrange("q (c p) -> q c p", c=2)

        def pair(t):
            return t[:, :].rearrange("q (c o p) -> q o c p", c=2, o=2)

        def pair_tok(t):
            return t[:, :].rearrange("q (p c o) -> q o c p", c=2, o=2)

        s_raw = [sem(f"raw_loaded{i}") for i in range(3)]
        s_zero = sem("stage_zeroed")
        s_const = sem("constants_made")
        s_ones = sem("ones_made")
        s_ids = sem("ids_loaded")
        s_rows = sem("rows_clamped")
        s_whi = sem("weight_hi_made")
        s_wlo = sem("weight_lo_made")
        s_gath = [sem(f"gathered{i}") for i in range(2)]
        s_rowc = sem("row_numbers_copied")
        s_gt = sem("pe_basin_transposed")
        s_gth = sem("basin_hi_made")
        s_gtl = sem("basin_lo_made")
        s_e = sem("pe_embedded")
        s_sq = sem("squares_summed")
        s_fw = sem("embedding_weighted")
        s_st = sem("stats_made")
        s_mv = sem("moments_made")
        s_ps = sem("pool_scale_steps")
        s_h = sem("residual_made")
        s_xn = sem("normed")
        s_xt = sem("pe_normed_transposed")
        s_xh = sem("normed_hi_made")
        s_xl = sem("normed_lo_made")
        s_qk = sem("pe_qk_made")
        s_qkh = sem("qk_hi_made")
        s_qkl = sem("qk_lo_made")
        s_v = sem("pe_v_made")
        s_vh = sem("v_hi_made")
        s_vl = sem("v_lo_made")
        s_s = sem("pe_scores_made")
        s_mx = sem("row_max_found")
        s_nb = sem("exp_bias_made")
        s_ex = sem("exps_made")
        s_ri = sem("row_sums_inverted")
        s_pn = sem("probabilities_made")
        s_pt = sem("pe_probabilities_transposed")
        s_pth = sem("probability_hi_made")
        s_ptl = sem("probability_lo_made")
        s_y = sem("pe_attended")
        s_yh = sem("attended_hi_made")
        s_yl = sem("attended_lo_made")
        s_wc = sem("pe_attention_out_made")
        s_h2 = sem("second_residual_made")
        s_st2 = sem("second_stats_made")
        s_mv2 = sem("second_moments_made")
        s_p2 = sem("pool_second_scale_steps")
        s_xn2 = sem("second_normed")
        s_zt = sem("pe_second_normed_transposed")
        s_zh = sem("second_normed_hi_made")
        s_zl = sem("second_normed_lo_made")
        s_rt = sem("pe_logits_made")
        s_re = sem("logit_exps_made")
        s_rc = sem("router_steps")
        s_comb = sem("combine_made")
        s_ct = sem("pe_combine_transposed")
        s_cs = sem("combine_copied")
        s_cd = sem("combine_stored")
        s_cb = [[sem(f"combine_spread{i}_{k}") for k in range(3)] for i in range(2)]
        s_up = sem("pe_up_made")
        s_r = sem("relu_made")
        s_t = sem("hidden_weighted")
        s_u = sem("hidden_squared")
        s_uh = sem("hidden_hi_made")
        s_ul = sem("hidden_lo_made")
        s_dn = sem("pe_down_made")
        s_ot = sem("output_made")
        s_out = sem("output_stored")
        NRC = 19

        GT_, E_, BN_, XN_, XT_, H_, QK_, V_, S_ = 0, 1, 2, 3, 4, 7, (6, 7, 8), (9, 10), (11, 12)
        PT_, Y_, WC_, XN2_, ZT_, RT_, CT_ = (0, 1), (2, 3), 5, 6, 7, 8, 10

        block = ctx.enter_context(nc.Block())

        def schedule(eng, step):
            step(Group(0, 0), None, None, None)
            step(Group(0, 1), Group(0, 0), None, None)
            step(Group(0, 2), Group(0, 1), Group(0, 0), None)
            step(Group(0, 3), Group(0, 2), Group(0, 1), Group(0, 0))
            with eng.Fori(1, STEPS // 2 - 1) as i:
                step(Group(i, 2), Group(i, 1), Group(i, 0), Group(i, -1))
                step(Group(i, 3), Group(i, 2), Group(i, 1), Group(i, 0))
            last = STEPS // 2 - 1
            step(None, Group(last, 1), Group(last, 0), Group(last, -1))
            step(None, None, Group(last, 1), Group(last, 0))
            step(None, None, None, Group(last, 1))

        def chunk_at(k, lag, m, t):
            return (k - lag, m) if k >= lag else (k - lag + NCH, t)

        @block.sync
        def _(sp):
            sp.dma_start(ids[:, :, :], ids_v).then_inc(s_ids, 16)
            for half in (0, KD):
                sp.dma_start(rPJ[half:half + KD, :], w_proj).then_inc(s_raw[0], 16)
            sp.dma_start(normw[:, :], norm_w.partition_broadcast(P)).then_inc(s_raw[0], 16)
            sp.dma_start(rQK0, w_qk[0:P, :]).then_inc(s_raw[1], 16)
            sp.dma_start(rWV0, w_v[0:P, :]).then_inc(s_raw[1], 16)
            sp.dma_start(rRW0, w_router[0:P, :]).then_inc(s_raw[1], 16)
            for half in (0, KD):
                sp.dma_start(rQK1[half:half + DR, :], w_qk[P:D, :]).then_inc(s_raw[1], 16)
                sp.dma_start(rWV1[half:half + DR, :], w_v[P:D, :]).then_inc(s_raw[1], 16)
                sp.dma_start(rRW1[half:half + DR, :], w_router[P:D, :]).then_inc(s_raw[1], 16)
            sp.dma_start(bqk[:, :], b_qk).then_inc(s_raw[1], 16)
            sp.dma_start(balb[:, :], b_bal.partition_broadcast(P)).then_inc(s_raw[1], 16)
            sp.wait_ge(s_zero, 2)
            sp.dma_start(rWC[:, 0:D], w_c[0:P, :]).then_inc(s_raw[1], 16)
            sp.dma_start(rWC[:, D:2 * D], w_c[KD:KD + P, :]).then_inc(s_raw[1], 16)
            sp.dma_start(rWC[0:KD, 2 * D:3 * D], w_c[P:D, :]).then_inc(s_raw[1], 16)
            sp.dma_start(rWC[KD:P, 3 * D:4 * D], w_c[0:KD, :]).then_inc(s_raw[1], 16)
            for row in (0, 32):
                sp.dma_start(rB[row:row + 1, 0:D], b_v.rearrange("(a n) -> a n", a=1)).then_inc(s_raw[1], 16)
                sp.dma_start(rB[row:row + 1, D:2 * D], b_c.rearrange("(a n) -> a n", a=1)).then_inc(s_raw[1], 16)
            sp.dma_start(rUP0, w_up[0:P, :]).then_inc(s_raw[2], 16)
            for half in (0, KD):
                sp.dma_start(rUP1[half:half + DR, :], w_up[P:D, :]).then_inc(s_raw[2], 16)
            sp.dma_start(rDN.rearrange("p (c n) -> p c n", c=NCH),
                         w_down.rearrange("(c p) n -> p c n", p=P)).then_inc(s_raw[2], 16)

            def step(a, b, m, t):
                if t is not None:
                    sp.wait_ge(s_ot, t.of(2, 2))
                    sp.dma_start(out_v[t.n, :, :], h2[t.par][:, :, :].rearrange("p r d -> p (r d)")).then_inc(s_out, 16)
                if b is not None:
                    sp.wait_ge(s_cs, b.of(1, 1))
                    for r in range(TR):
                        sp.dma_start(comb_dram[b.par][:, r * P:(r + 1) * P],
                                     combT[P - (TR - r) * NE:P - (TR - r - 1) * NE, :]).then_inc(s_cd, 16)
                    sp.wait_ge(s_cd, b.of(16 * TR, 16 * TR))
                    cb, pairs = combB[b.par], comb_dram[b.par].rearrange("(g o) t -> o g t", o=2)
                    for k, (lo, hi, j, odd) in enumerate(((0, P, 0, 0), (0, KD, 1, 0), (KD, P, 1, 1), (0, P, 2, 1))):
                        sp.dma_start(cb[lo:hi, j:ECH:3, :], pairs[odd].partition_broadcast(hi - lo))\
                          .then_inc(s_cb[b.par][(k + 1) // 2], 16)

            schedule(sp, step)
            sp.wait_ge(s_out, 16 * STEPS)

        @block.gpsimd
        def _(pool):
            pool.memset(rWC, 0.0).then_inc(s_zero, 1)
            pool.memset(rB, 0.0).then_inc(s_zero, 1)
            pool.memset(ident[:, :], 0.0).then_inc(s_const, 1)
            pool.wait_ge(s_const, 1)
            pool.affine_select(out=ident[:, :], in_=ident[:, :], compare_op=ALU.not_equal, fill=1.0, base=0,
                               pattern=[[-1, P]], channel_multiplier=1).then_inc(s_const, 1)
            pool.memset(nhalf[:, :], -0.5).then_inc(s_const, 1)
            for e in range(NE):
                pool.memset(rank[:, :, e:e + 1], float(NE - e)).then_inc(s_const, 1)

            def gather(g, first):
                pool.tensor_copy(row_now[g.par][:, :], rows[:, g.n, :]).then_inc(s_rowc, 1)
                pool.wait_ge(s_rowc, g.of(1, 1))
                if not first:
                    pool.wait_ge(s_gt, g.of(1, -1))
                for r in range(TR):
                    pool.indirect_dma_start(out=G[g.par][:, r, :], out_offset=None, in_=coords,
                                            in_offset=bass.IndirectOffsetOnAxis(ap=row_now[g.par][:, r:r + 1], axis=0))\
                        .then_inc(s_gath[g.par], 16)

            pool.wait_ge(s_rows, 5)
            gather(Group(0, 0), True)

            def step(a, b, m, t):
                for k in range(NCH):
                    if m is not None and k < ECH:
                        if k < 3:
                            n = 32 if k == 1 else 16
                            pool.wait_ge(s_cb[m.par][k], m.half * n + n)
                        pool.wait_ge(s_r, m.of(NCH, k + 1))
                        if t is not None or k >= 2:
                            pool.wait_ge(s_ul, m.of(NCH, k - 1))
                        pool.tensor_tensor(U[k % 2][:, :], R[k % 2][:, :], combB[m.par][:, k, :], ALU.mult)\
                            .then_inc(s_t, 1)
                    if a is not None and k == BN_:
                        c = 0

                        def link(ins):
                            nonlocal c
                            c += 1
                            ins.then_inc(s_ps, 1)

                        pool.wait_ge(s_sq, a.of(2, 2))
                        link(pool.tensor_scalar(sA[:, 0, :], ss[:, :], 1.0 / D, EPS_RMS, ALU.mult, ALU.add))
                        pool.wait_ge(s_ps, a.of(7, c))
                        link(pool.tensor_tensor(sr1[:, :], sA[:, 0, :], nhalf[:, :], ALU.pow))
                        pool.wait_ge(s_ps, a.of(7, c))
                        link(pool.tensor_tensor(sA[:, 1, :], sr1[:, :], sr1[:, :], ALU.mult))
                        pool.wait_ge(s_ps, a.of(7, c))
                        pool.wait_ge(s_mv, a.of(3, 3))
                        link(pool.tensor_tensor(sA[:, 2, :], sA[:, 1, :], mm[:, 5, :], ALU.mult))
                        pool.wait_ge(s_ps, a.of(7, c))
                        link(pool.tensor_scalar(sA[:, 3, :], sA[:, 2, :], 1.0 / D, EPS_LN, ALU.mult, ALU.add))
                        pool.wait_ge(s_ps, a.of(7, c))
                        link(pool.tensor_tensor(sA[:, 0, :], sA[:, 3, :], nhalf[:, :], ALU.pow))
                        pool.wait_ge(s_ps, a.of(7, c))
                        link(pool.tensor_tensor(sscl[:, :], sA[:, 0, :], sr1[:, :], ALU.mult))
                        assert c == 7
                    if a is not None and k == H_:
                        if b is not None:
                            pool.wait_ge(s_h2, b.of(2, 2))
                        for r in range(TR):
                            last = pool.tensor_scalar(h[:, r, :], Fw[:, r, :], sr1[:, r:r + 1], None, ALU.mult)
                        last.then_inc(s_h, 1)
                    if b is not None and k == XN2_:
                        pool.wait_ge(s_mv2, b.of(3, 3))
                        pool.tensor_scalar(ve2[:, :], mm2[:, 5, :], 1.0 / D, EPS_LN, ALU.mult, ALU.add).then_inc(s_p2, 1)
                        pool.wait_ge(s_p2, b.of(2, 1))
                        pool.tensor_tensor(s2[:, :], ve2[:, :], nhalf[:, :], ALU.pow).then_inc(s_p2, 1)

            def group_then_gather(eng):
                step(Group(0, 0), None, None, None)
                gather(Group(0, 1), True)
                step(Group(0, 1), Group(0, 0), None, None)
                gather(Group(0, 2), False)
                step(Group(0, 2), Group(0, 1), Group(0, 0), None)
                gather(Group(0, 3), False)
                step(Group(0, 3), Group(0, 2), Group(0, 1), Group(0, 0))
                gather(Group(0, 4), False)
                with eng.Fori(1, STEPS // 2 - 2) as i:
                    step(Group(i, 2), Group(i, 1), Group(i, 0), Group(i, -1))
                    gather(Group(i, 3), False)
                    step(Group(i, 3), Group(i, 2), Group(i, 1), Group(i, 0))
                    gather(Group(i, 4), False)
                i = STEPS // 2 - 2
                step(Group(i, 2), Group(i, 1), Group(i, 0), Group(i, -1))
                gather(Group(i, 3), False)
                step(Group(i, 3), Group(i, 2), Group(i, 1), Group(i, 0))
                last = STEPS // 2 - 1
                step(None, Group(last, 1), Group(last, 0), Group(last, -1))
                step(None, None, Group(last, 1), Group(last, 0))

            group_then_gather(pool)

        def pieces(rawt, hi, lo, n, w=GT):
            return [(rawt[:, c:min(c + w, n)], hi[:, c:min(c + w, n)], lo[:, c:min(c + w, n)]) for c in range(0, n, w)]

        flatC = [t[:, :, :].rearrange("p a b -> p (a b)") for t in (WCh, WCl)]
        flatD = [t[:, :, :].rearrange("p a b -> p (a b)") for t in (DNh, DNl)]
        first_w = pieces(rPJ, PJh, PJl, D)
        small_w = (pieces(rQK0, QK0h, QK0l, 2 * D) + pieces(rQK1, QK1h, QK1l, 2 * D) +
                   pieces(rWV0, WV0h, WV0l, D) + pieces(rWV1, WV1h, WV1l, D) +
                   pieces(rWC, flatC[0], flatC[1], 4 * D, 4 * D) +
                   pieces(rRW0, RW0h, RW0l, NE) + pieces(rRW1, RW1h, RW1l, NE))
        big_w = pieces(rUP0, UP0h, UP0l, HP) + pieces(rUP1, UP1h, UP1l, HP) + pieces(rDN, flatD[0], flatD[1], NCH * D)
        RAW1 = 16 * (3 + 6 + 2 + 4 + 4)
        RAW2 = 16 * 4
        n_first, n_small, n_big = len(first_w), len(small_w), len(big_w)
        slot_w = [big_w[k * n_big // NCH:(k + 1) * n_big // NCH] for k in range(NCH)]

        @block.scalar
        def _(act):
            act.preload_act_table(ACT.Exp)
            act.wait_ge(s_raw[0], 48)
            for src, hi, lo in first_w:
                act.activation(hi, src, ACT.Copy).then_inc(s_whi, 1)
            act.wait_ge(s_raw[1], RAW1)
            for src, hi, lo in small_w:
                act.activation(hi, src, ACT.Copy).then_inc(s_whi, 1)
            act.activation(BVC[:, :], rB, ACT.Copy).then_inc(s_whi, 1)
            act.wait_ge(s_raw[2], RAW2)

            def step(a, b, m, t):
                for k in range(NCH):
                    if a is not None and b is None:
                        for src, hi, lo in slot_w[k]:
                            act.activation(hi, src, ACT.Copy).then_inc(s_whi, 1)
                    if m is not None:
                        act.wait_ge(s_up, m.of(NCH, k + 1))
                        if t is not None or k >= 2:
                            act.wait_ge(s_u, m.of(NCH, k - 1))
                        act.activation(R[k % 2][:, :], UB[k % 2][:, :], ACT.Relu).then_inc(s_r, 1)
                    j, g = chunk_at(k, 2, m, t)
                    if g is not None:
                        act.wait_ge(s_u, g.of(NCH, j + 1))
                        if not (isinstance(g.n, int) and g.n == 0 and j < 2):
                            act.wait_ge(s_dn, g.of(NCH, j - 1))
                        act.activation(Uh[j % 2][:, :], U[j % 2][:, :], ACT.Copy).then_inc(s_uh, 1)
                    if a is not None:
                        if k == GT_:
                            act.wait_ge(s_gt, a.of(1, 1))
                            for o in range(2):
                                last = act.activation(pair(GTs)[0:KD, o], halves(A[0])[o * KD:(o + 1) * KD], ACT.Copy)
                            last.then_inc(s_gth, 1)
                        if k == E_:
                            for c in range(2):
                                act.wait_ge(s_e, a.of(2, c + 1))
                                for r in range(2):
                                    last = act.activation(xn[:, c, r * D:(r + 1) * D], A[1 - c][:, r * D:(r + 1) * D], ACT.Square,
                                                          accum_out=ss[:, 2 * c + r:2 * c + r + 1])
                                last.then_inc(s_sq, 1)
                        if k == XT_:
                            act.wait_ge(s_xt, a.of(2, 1))
                            act.activation(X0h[:, :].rearrange("q (p r) -> q p r", r=TR),
                                           A[1][:, :].rearrange("q (r p) -> q p r", r=TR), ACT.Copy).then_inc(s_xh, 1)
                            act.wait_ge(s_xt, a.of(2, 2))
                            for o in range(2):
                                last = act.activation(pair_tok(X1)[0:DR, o], halves(A[0])[o * DR:(o + 1) * DR], ACT.Copy)
                            last.then_inc(s_xh, 1)
                        if k == QK_[0]:
                            act.wait_ge(s_qk, a.of(3, 1))
                            act.activation(Q0h[:, :], A[1][:, :], ACT.Identity, bias=bqk[:, 0:1]).then_inc(s_qkh, 1)
                        if k == QK_[1]:
                            act.wait_ge(s_qk, a.of(3, 2))
                            act.activation(K0h[:, :], A[0][:, :], ACT.Identity, bias=bqk[:, 1:2]).then_inc(s_qkh, 1)
                        if k == QK_[2]:
                            act.wait_ge(s_qk, a.of(3, 3))
                            act.activation(K1h[0:KD, :], A[1][KD:P, :], ACT.Identity, bias=bqk[KD:P, 2:3])
                            act.activation(K1h[KD:P, :], A[1][KD:P, :], ACT.Identity, bias=bqk[KD:P, 2:3])
                            act.activation(Q1[0:KD, :], A[1][0:KD, :], ACT.Identity, bias=bqk[0:KD, 2:3])\
                               .then_inc(s_qkh, 1)
                        for c in range(2):
                            if k == V_[c]:
                                act.wait_ge(s_v, a.of(2, c + 1))
                                act.activation(Vh[:, 2 * c:2 * c + 2, :], two(A[c]), ACT.Copy).then_inc(s_vh, 1)
                            if k == S_[c]:
                                act.wait_ge(s_nb, a.of(2, c + 1))
                                for q in range(QT):
                                    last = act.activation(Pr[:, c, q, :], B[c][:, q * SEQ:(q + 1) * SEQ], ACT.Exp,
                                                          bias=nb[:, c, q:q + 1], scale=SCALE,
                                                          accum_out=rs[:, c, q:q + 1])
                                last.then_inc(s_ex, 1)
                    if b is not None:
                        for c in range(2):
                            if k == PT_[c]:
                                act.wait_ge(s_pt, b.of(2, c + 1))
                                act.activation(PTh[:, c, :, :], B[c][:, :].rearrange("p (t q) -> p t q", t=QT), ACT.Copy)\
                                   .then_inc(s_pth, 1)
                            if k == Y_[c]:
                                act.wait_ge(s_y, b.of(2, c + 1))
                                for q in range(QT):
                                    last = act.activation(Yh[:, q, :, c, :],
                                                          two(B[c])[:, q, :].rearrange("p (a c) -> p c a", c=3), ACT.Copy)
                                last.then_inc(s_yh, 1)
                        if k == ZT_:
                            act.wait_ge(s_zt, b.of(2, 1))
                            act.activation(Z0h[b.par][:, :], B[0][:, :], ACT.Copy).then_inc(s_zh, 1)
                            act.wait_ge(s_zt, b.of(2, 2))
                            for o in range(2):
                                last = act.activation(pair(Z1[b.par])[0:DR, o], halves(B[1])[o * DR:(o + 1) * DR], ACT.Copy)
                            last.then_inc(s_zh, 1)
                        if k == RT_:
                            act.wait_ge(s_rt, b.of(1, 1))
                            act.activation(rt[:, 0, :, :].rearrange("p r e -> p (r e)"), B[0][:, 0:TR * NE], ACT.Exp,
                                           scale=-1.0).then_inc(s_re, 1)
                        if k == CT_:
                            act.wait_ge(s_ct, b.of(1, 1))
                            if not (isinstance(b.n, int) and b.n == 0):
                                act.wait_ge(s_cd, b.of(16 * TR, 0))
                            act.activation(combT[P - TR * NE:P, :], B[1][P - TR * NE:P, 0:P], ACT.Copy).then_inc(s_cs, 1)

            schedule(act, step)

        @block.vector
        def _(dve):
            dve.memset(ones[:, :].bitcast(f32), 1.0).then_inc(s_ones, 1)
            dve.memset(K1l[KD:P, :].bitcast(f32), 0.0).then_inc(s_ones, 1)
            dve.wait_ge(s_ids, 16)
            dve.tensor_copy(idf[:, :, :], ids[:, :, :]).then_inc(s_rows, 1)
            dve.wait_ge(s_rows, 1)
            dve.tensor_scalar(neg[:, :, :], idf[:, :, :], 0.0, float(VOCAB), ALU.is_lt, ALU.mult).then_inc(s_rows, 1)
            dve.wait_ge(s_rows, 2)
            dve.tensor_tensor(neg[:, :, :], idf[:, :, :], neg[:, :, :], ALU.add).then_inc(s_rows, 1)
            dve.wait_ge(s_rows, 3)
            dve.tensor_scalar(idf[:, :, :], neg[:, :, :], 0.0, float(VOCAB - 1), ALU.max, ALU.min).then_inc(s_rows, 1)
            dve.wait_ge(s_rows, 4)
            dve.tensor_copy(rows[:, :, :], idf[:, :, :]).then_inc(s_rows, 1)
            made = 0
            for src, hi, lo in first_w + small_w:
                made += 1
                dve.wait_ge(s_whi, made)
                dve.tensor_tensor(lo, src, hi.bitcast(f32), ALU.subtract).then_inc(s_wlo, 1)
            dve.wait_ge(s_whi, made + 1)
            dve.tensor_tensor(BVC[32:33, :], rB[32:33, :], BVC[32:33, :].bitcast(f32), ALU.subtract).then_inc(s_wlo, 1)

            def step(a, b, m, t):
                first = a is not None and b is None
                done = n_first + n_small + 1
                for k in range(NCH):
                    if first:
                        for src, hi, lo in slot_w[k]:
                            done += 1
                            dve.wait_ge(s_whi, done)
                            dve.tensor_tensor(lo, src, hi.bitcast(f32), ALU.subtract).then_inc(s_wlo, 1)
                    j, g = chunk_at(k, 1, m, t)
                    if g is not None:
                        if j < ECH:
                            dve.wait_ge(s_t, g.of(ECH, j + 1))
                            other = U[j % 2]
                        else:
                            dve.wait_ge(s_r, g.of(NCH, j + 1))
                            dve.wait_ge(s_ul, g.of(NCH, j - 1))
                            other = R[j % 2]
                        dve.tensor_tensor(U[j % 2][:, :], other[:, :], R[j % 2][:, :], ALU.mult).then_inc(s_u, 1)
                    j, g = chunk_at(k, 2, m, t)
                    if g is not None:
                        dve.wait_ge(s_uh, g.of(NCH, j + 1))
                        dve.tensor_tensor(Ul[j % 2][:, :], U[j % 2][:, :], Uh[j % 2][:, :].bitcast(f32), ALU.subtract)\
                           .then_inc(s_ul, 1)
                    if t is not None and k == LAG:
                        dve.wait_ge(s_dn, t.of(NCH, NCH))
                        for c in range(2):
                            dve.tensor_tensor(h2[t.par][:, 2 * c:2 * c + 2, :], two(AC[c]), h2[t.par][:, 2 * c:2 * c + 2, :], ALU.add)\
                               .then_inc(s_ot, 1)
                    if a is not None:
                        if k == GT_:
                            dve.wait_ge(s_gth, a.of(1, 1))
                            for o in range(2):
                                last = dve.tensor_tensor(pair(GTs)[KD:P, o], halves(A[0])[o * KD:(o + 1) * KD],
                                                         pair(GTs)[0:KD, o].bitcast(f32), ALU.subtract)
                            last.then_inc(s_gtl, 1)
                        if k == E_:
                            if not (isinstance(a.n, int) and a.n == 0):
                                dve.wait_ge(s_h, a.of(1, 0))
                            for c in range(2):
                                dve.wait_ge(s_sq, a.of(2, c + 1))
                                dve.tensor_tensor(Fw[:, 2 * c:2 * c + 2, :], two(A[1 - c]),
                                                  normw[:, :].unsqueeze(1).to_broadcast([P, 2, D]), ALU.mult).then_inc(s_fw, 1)
                            dve.wait_ge(s_fw, a.of(2, 2))
                            for r in range(TR):
                                last = dve.bn_stats(st[:, r, :], Fw[:, r, :])
                            last.then_inc(s_st, 1)
                            moments(a, st, mm, s_st, s_mv)
                        if k == XN_:
                            dve.wait_ge(s_ps, a.of(7, 7))
                            normed(Fw, mm[:, 3, :], sscl).then_inc(s_xn, 1)
                        if k == XT_:
                            dve.wait_ge(s_xh, a.of(2, 1))
                            dve.tensor_tensor(X0l[:, :].rearrange("q (p r) -> q p r", r=TR),
                                              A[1][:, :].rearrange("q (r p) -> q p r", r=TR),
                                              X0h[:, :].bitcast(f32).rearrange("q (p r) -> q p r", r=TR),
                                              ALU.subtract).then_inc(s_xl, 1)
                            dve.wait_ge(s_xh, a.of(2, 2))
                            for o in range(2):
                                last = dve.tensor_tensor(pair_tok(X1)[DR:P, o], halves(A[0])[o * DR:(o + 1) * DR],
                                                         pair_tok(X1)[0:DR, o].bitcast(f32), ALU.subtract)
                            last.then_inc(s_xl, 1)
                        if k == QK_[0]:
                            dve.wait_ge(s_qkh, a.of(3, 1))
                            dve.scalar_tensor_tensor(Q0l[:, :], A[1][:, :], bqk[:, 0:1], Q0h[:, :].bitcast(f32),
                                                     ALU.add, ALU.subtract).then_inc(s_qkl, 1)
                        if k == QK_[1]:
                            dve.wait_ge(s_qkh, a.of(3, 2))
                            dve.scalar_tensor_tensor(K0l[:, :], A[0][:, :], bqk[:, 1:2], K0h[:, :].bitcast(f32),
                                                     ALU.add, ALU.subtract).then_inc(s_qkl, 1)
                        if k == QK_[2]:
                            dve.wait_ge(s_qkh, a.of(3, 3))
                            dve.scalar_tensor_tensor(K1l[0:KD, :], A[1][KD:P, :], bqk[KD:P, 2:3],
                                                     K1h[KD:P, :].bitcast(f32), ALU.add, ALU.subtract)
                            dve.scalar_tensor_tensor(Q1[KD:P, :], A[1][0:KD, :], bqk[0:KD, 2:3],
                                                     Q1[0:KD, :].bitcast(f32), ALU.add, ALU.subtract).then_inc(s_qkl, 1)
                        for c in range(2):
                            if k == V_[c]:
                                dve.wait_ge(s_vh, a.of(2, c + 1))
                                dve.tensor_tensor(Vl[:, 2 * c:2 * c + 2, :], two(A[c]),
                                                  Vh[:, 2 * c:2 * c + 2, :].bitcast(f32), ALU.subtract).then_inc(s_vl, 1)
                            if k == S_[c]:
                                dve.wait_ge(s_s, a.of(2, c + 1))
                                dve.tensor_reduce(mx[:, c, :], B[c][:, :].rearrange("p (q s) -> p q s", q=QT), AX.X, ALU.max)\
                                   .then_inc(s_mx, 1)
                                dve.wait_ge(s_mx, a.of(2, c + 1))
                                dve.tensor_scalar(nb[:, c, :], mx[:, c, :], -SCALE, None, ALU.mult).then_inc(s_nb, 1)
                                dve.wait_ge(s_ex, a.of(2, c + 1))
                                dve.reciprocal(ri[:, c, :], rs[:, c, :]).then_inc(s_ri, 1)
                                dve.wait_ge(s_ri, a.of(2, c + 1))
                                for q in range(QT):
                                    last = dve.tensor_scalar(Pr[:, c, q, :], Pr[:, c, q, :], ri[:, c, q:q + 1], None, ALU.mult)
                                last.then_inc(s_pn, 1)
                    if b is not None:
                        for c in range(2):
                            if k == PT_[c]:
                                dve.wait_ge(s_pth, b.of(2, c + 1))
                                dve.tensor_tensor(PTl[:, c, :, :], B[c][:, :].rearrange("p (t q) -> p t q", t=QT),
                                                  PTh[:, c, :, :].bitcast(f32), ALU.subtract).then_inc(s_ptl, 1)
                            if k == Y_[c]:
                                dve.wait_ge(s_yh, b.of(2, c + 1))
                                for q in range(QT):
                                    last = dve.tensor_tensor(Yl[:, q, :, c, :],
                                                             two(B[c])[:, q, :].rearrange("p (a c) -> p c a", c=3),
                                                             Yh[:, q, :, c, :].bitcast(f32), ALU.subtract)
                                last.then_inc(s_yl, 1)
                        if k == WC_:
                            dve.wait_ge(s_h, b.of(1, 1))
                            if t is not None:
                                dve.wait_ge(s_out, t.of(16, 16))
                            for c in range(2):
                                dve.wait_ge(s_wc, b.of(2, c + 1))
                                dve.tensor_tensor(h2[b.par][:, 2 * c:2 * c + 2, :], two(B[c]),
                                                  h[:, 2 * c:2 * c + 2, :], ALU.add).then_inc(s_h2, 1)
                            dve.wait_ge(s_h2, b.of(2, 2))
                            for r in range(TR):
                                last = dve.bn_stats(st2[:, r, :], h2[b.par][:, r, :])
                            last.then_inc(s_st2, 1)
                            moments(b, st2, mm2, s_st2, s_mv2)
                        if k == XN2_:
                            dve.wait_ge(s_p2, b.of(2, 2))
                            normed(h2[b.par], mm2[:, 3, :], s2).then_inc(s_xn2, 1)
                        if k == ZT_:
                            dve.wait_ge(s_zh, b.of(2, 1))
                            dve.tensor_tensor(Z0l[b.par][:, :], B[0][:, :], Z0h[b.par][:, :].bitcast(f32), ALU.subtract)\
                               .then_inc(s_zl, 1)
                            dve.wait_ge(s_zh, b.of(2, 2))
                            for o in range(2):
                                last = dve.tensor_tensor(pair(Z1[b.par])[DR:P, o], halves(B[1])[o * DR:(o + 1) * DR],
                                                         pair(Z1[b.par])[0:DR, o].bitcast(f32), ALU.subtract)
                            last.then_inc(s_zl, 1)
                        if k == RT_:
                            route(b)

            def normed(src, mean, scale):
                for r in range(TR):
                    c, odd = r // 2, r % 2
                    for lo, hi, at in (((0, P, 2 * P), (P, D, D)) if odd else ((0, D, 0),)):
                        last = dve.tensor_scalar(xn[:, c, at:at + hi - lo], src[:, r, lo:hi], mean[:, r:r + 1],
                                                 scale[:, r:r + 1], ALU.subtract, ALU.mult)
                return last

            def moments(g, stats, to, s_in, s_to):
                dve.wait_ge(s_in, g.of(1, 1))
                dve.tensor_tensor(to[:, 0, :], stats[:, :, 1], stats[:, :, 4], ALU.add)
                dve.tensor_tensor(to[:, 1, :], stats[:, :, 1], stats[:, :, 4], ALU.subtract)
                dve.tensor_tensor(to[:, 2, :], stats[:, :, 2], stats[:, :, 5], ALU.add).then_inc(s_to, 1)
                dve.wait_ge(s_to, g.of(3, 1))
                dve.tensor_scalar(to[:, 3, :], to[:, 0, :], 0.5, None, ALU.mult)
                dve.tensor_tensor(to[:, 4, :], to[:, 1, :], to[:, 1, :], ALU.mult).then_inc(s_to, 1)
                dve.wait_ge(s_to, g.of(3, 2))
                dve.scalar_tensor_tensor(to[:, 5, :], to[:, 4, :], D / 4.0, to[:, 2, :], ALU.mult, ALU.add).then_inc(s_to, 1)

            def route(b):
                c = 0

                def link(ins):
                    nonlocal c
                    c += 1
                    ins.then_inc(s_rc, 1)
                    dve.wait_ge(s_rc, b.of(NRC, c))

                def wide(i):
                    return rm[:, i, :].unsqueeze(2).to_broadcast([P, TR, NE])

                dve.wait_ge(s_re, b.of(1, 1))
                link(dve.tensor_scalar(rt[:, 1, :, :], rt[:, 0, :, :], 1.0, None, ALU.add))
                link(dve.reciprocal(rt[:, 2, :, :], rt[:, 1, :, :]))
                link(dve.tensor_tensor(rt[:, 3, :, :], rt[:, 2, :, :],
                                       balb[:, :].unsqueeze(1).to_broadcast([P, TR, NE]), ALU.add))
                sel = 3
                for one in range(2):
                    s = 4 + 4 * one
                    link(dve.tensor_reduce(rm[:, 2 * one, :], rt[:, sel, :, :], AX.X, ALU.max))
                    link(dve.tensor_tensor(rt[:, s, :, :], rt[:, sel, :, :], wide(2 * one), ALU.is_equal))
                    link(dve.tensor_tensor(rt[:, s + 1, :, :], rt[:, s, :, :], rank[:, :, :], ALU.mult))
                    link(dve.tensor_reduce(rm[:, 2 * one + 1, :], rt[:, s + 1, :, :], AX.X, ALU.max))
                    link(dve.tensor_tensor(rt[:, s + 2, :, :], rt[:, s + 1, :, :], wide(2 * one + 1), ALU.is_equal))
                    if one == 0:
                        link(dve.scalar_tensor_tensor(rt[:, 7, :, :], rt[:, 6, :, :], -BIG, rt[:, 3, :, :], ALU.mult, ALU.add))
                        sel = 7
                link(dve.tensor_tensor(rt[:, 11, :, :], rt[:, 6, :, :], rt[:, 10, :, :], ALU.add))
                link(dve.tensor_tensor(rt[:, 12, :, :], rt[:, 11, :, :], rt[:, 2, :, :], ALU.mult))
                link(dve.tensor_reduce(rm[:, 4, :], rt[:, 12, :, :], AX.X, ALU.add))
                link(dve.tensor_scalar(rm[:, 4, :], rm[:, 4, :], EPS_TOP, None, ALU.add))
                dve.reciprocal(rm[:, 5, :], rm[:, 4, :]).then_inc(s_rc, 1)
                c += 1
                dve.wait_ge(s_rc, b.of(NRC, c))
                dve.tensor_tensor(rt[:, 13, :, :], rt[:, 12, :, :], wide(5), ALU.mult).then_inc(s_comb, 1)
                assert c == NRC, c

            schedule(dve, step)

        @block.tensor
        def _(pe):
            ident_r = ident[:, :]
            pe.wait_ge(s_const, 11)
            pe.wait_ge(s_ones, 2)

            def split5(dst, s0h, s0l, s1, mvh, mvl, m1h, m1l, start, stop, tail=None):
                pe.matmul(dst, s0h, mvh, start=start, stop=False, skip_group_check=True)
                pe.matmul(dst, s0h, mvl, start=False, stop=False, skip_group_check=True)
                pe.matmul(dst, s0l, mvh, start=False, stop=False, skip_group_check=True)
                pe.matmul(dst, s1, m1h, start=False, stop=False, skip_group_check=True)
                last = pe.matmul(dst, s1, m1l, start=False, stop=stop and tail is None, skip_group_check=True)
                if tail is not None:
                    last = pe.matmul(dst, tail[0], tail[1], start=False, stop=stop, skip_group_check=True)
                return last

            def weights5(dst, w0h, w0l, w1h, w1l, xh, xl, x1):
                pe.matmul(dst, w0h, xh, start=True, stop=False)
                pe.matmul(dst, w0h, xl, start=False, stop=False)
                pe.matmul(dst, w0l, xh, start=False, stop=False)
                pe.matmul(dst, w1h, x1, start=False, stop=False)
                return pe.matmul(dst, w1l, x1, start=False, stop=True)

            def stage_a(a, k):
                later = not (isinstance(a.n, int) and a.n == 0)
                if k == GT_:
                    pe.wait_ge(s_gath[a.par], a.half * 64 + 64)
                    if later:
                        pe.wait_ge(s_vl, a.of(2, -1))
                    for c in range(2):
                        last = pe.transpose(A[0][:, c * P:(c + 1) * P],
                                            G[a.par][:, 2 * c:2 * c + 2, :].rearrange("p r k -> p (r k)"), ident_r)
                    last.then_inc(s_gt, 1)
                if k == E_:
                    if not later:
                        pe.wait_ge(s_wlo, n_first)
                    else:
                        pe.wait_ge(s_vl, a.of(2, 0))
                    pe.wait_ge(s_gtl, a.of(1, 1))
                    for c in range(2):
                        for r in range(2):
                            dst = two(A[1 - c])[:, r, :]
                            lhs = GTs[:, (2 * c + r) * P:(2 * c + r + 1) * P]
                            pe.matmul(dst, lhs, PJh[:, :], start=True, stop=False)
                            last = pe.matmul(dst, lhs, PJl[:, :], start=False, stop=True)
                        last.then_inc(s_e, 1)
                if k == XT_:
                    pe.wait_ge(s_xn, a.of(1, 1))
                    for r in range(TR):
                        last = pe.transpose(A[1][:, r * P:(r + 1) * P], xn[:, r // 2, r % 2 * 2 * P:r % 2 * 2 * P + P], ident_r)
                    last.then_inc(s_xt, 1)
                    for c in range(2):
                        last = pe.transpose(A[0][:, c * P:(c + 1) * P], xn[:, c, P:2 * P], ident_r)
                    last.then_inc(s_xt, 1)
                if k in QK_:
                    c = QK_.index(k)
                    if c == 0:
                        if not later:
                            pe.wait_ge(s_wlo, n_first + n_small + 1)
                        pe.wait_ge(s_xl, a.of(2, 2))
                    if c == 2:
                        pe.wait_ge(s_qkl, a.of(3, 1))
                    cols = slice(c * P, (c + 1) * P)
                    weights5(A[(1 + c) % 2][:, :], QK0h[:, cols], QK0l[:, cols], QK1h[:, cols], QK1l[:, cols],
                             X0h[:, :], X0l[:, :], X1[:, :]).then_inc(s_qk, 1)
                if k in V_:
                    c = V_.index(k)
                    pe.wait_ge(s_qkl, a.of(3, 2 + c))
                    for r in range(2):
                        tok = slice((2 * c + r) * P, (2 * c + r + 1) * P)
                        last = split5(two(A[c])[:, r, :], X0h[:, tok], X0l[:, tok], X1[:, tok], WV0h[:, :], WV0l[:, :],
                                      WV1h[:, :], WV1l[:, :], True, True, tail=(ones[:, :], BVC[:, 0:D]))
                    last.then_inc(s_v, 1)
                if k in S_:
                    c = S_.index(k)
                    pe.wait_ge(s_qkl, a.of(3, 3))
                    if later:
                        pe.wait_ge(s_re if c == 0 else s_cs, a.of(1, 0))
                    for q in range(QT):
                        qs = slice(c * SEQ + q * P, c * SEQ + (q + 1) * P)
                        ks = slice(c * SEQ, (c + 1) * SEQ)
                        last = split5(B[c][:, q * SEQ:(q + 1) * SEQ], Q0h[:, qs], Q0l[:, qs], Q1[:, qs], K0h[:, ks],
                                      K0l[:, ks], K1h[:, ks], K1l[:, ks], True, True)
                    last.then_inc(s_s, 1)

            WC_UNITS = [[(0, 0, 0), (1, 0, 2)], [(1, 0, 3), (0, 1, 1)], [(1, 1, 0), (0, 2, 2)], [(0, 2, 3), (1, 2, 1)]]

            def stage_b(b, k):
                if k in PT_:
                    c = PT_.index(k)
                    pe.wait_ge(s_pn, b.of(2, c + 1))
                    for q in range(QT):
                        for kt in range(QT):
                            last = pe.transpose(B[c][:, kt * SEQ + q * P:kt * SEQ + (q + 1) * P],
                                                Pr[:, c, q, kt * P:(kt + 1) * P], ident_r)
                    last.then_inc(s_pt, 1)
                if k in Y_:
                    c = Y_.index(k)
                    pe.wait_ge(s_ptl, b.of(2, c + 1))
                    pe.wait_ge(s_vl, b.of(2, 2))
                    for q in range(QT):
                        dst = two(B[c])[:, q, :]
                        for kt in range(QT):
                            qs, v = slice(q * P, (q + 1) * P), c * QT + kt
                            pe.matmul(dst, PTh[:, c, kt, qs], Vh[:, v, :], start=kt == 0, stop=False, skip_group_check=True)
                            pe.matmul(dst, PTh[:, c, kt, qs], Vl[:, v, :], start=False, stop=False, skip_group_check=True)
                            last = pe.matmul(dst, PTl[:, c, kt, qs], Vh[:, v, :], start=False, stop=kt == QT - 1,
                                             skip_group_check=True)
                    last.then_inc(s_y, 1)
                if k == WC_:
                    pe.wait_ge(s_yl, b.of(2, 2))
                    for c in range(2):
                        for r in range(2):
                            dst = two(B[c])[:, r, :]
                            for n, (qt, e3, w) in enumerate(WC_UNITS[2 * c + r]):
                                yh = Yh[:, qt, e3, :, :].rearrange("p s a -> p (s a)")
                                yl = Yl[:, qt, e3, :, :].rearrange("p s a -> p (s a)")
                                pe.matmul(dst, yh, WCh[:, w, :], start=n == 0, stop=False, skip_group_check=True)
                                pe.matmul(dst, yh, WCl[:, w, :], start=False, stop=False, skip_group_check=True)
                                pe.matmul(dst, yl, WCh[:, w, :], start=False, stop=False, skip_group_check=True)
                            last = pe.matmul(dst, ones[:, :], BVC[:, D:2 * D], start=False, stop=True, skip_group_check=True)
                        last.then_inc(s_wc, 1)
                if k == ZT_:
                    pe.wait_ge(s_xn2, b.of(1, 1))
                    for r in range(TR):
                        last = pe.transpose(B[0][:, r * P:(r + 1) * P], xn[:, r // 2, r % 2 * 2 * P:r % 2 * 2 * P + P], ident_r)
                    last.then_inc(s_zt, 1)
                    for c in range(2):
                        last = pe.transpose(B[1][:, c * P:(c + 1) * P], xn[:, c, P:2 * P], ident_r)
                    last.then_inc(s_zt, 1)
                if k == RT_:
                    pe.wait_ge(s_zl, b.of(2, 2))
                    z0h, z0l, z1 = Z0h[b.par], Z0l[b.par], Z1[b.par]
                    for r in range(TR):
                        tok = slice(r * P, (r + 1) * P)
                        last = split5(B[0][:, r * NE:(r + 1) * NE], z0h[:, tok], z0l[:, tok], z1[:, tok], RW0h[:, :],
                                      RW0l[:, :], RW1h[:, :], RW1l[:, :], True, True)
                    last.then_inc(s_rt, 1)
                if k == CT_:
                    pe.wait_ge(s_comb, b.of(1, 1))
                    pe.transpose(B[1][:, 0:P], rt[:, 10:14, :, :].rearrange("p i r e -> p (i r e)"), ident_r)\
                      .then_inc(s_ct, 1)

            def step(a, b, m, t):
                for k in range(NCH):
                    if m is not None:
                        if k == 0:
                            pe.wait_ge(s_zl, m.of(2, 2))
                            if t is None:
                                pe.wait_ge(s_wlo, n_first + n_small + 1 + n_big)
                        if t is not None or k >= 2:
                            pe.wait_ge(s_r, m.of(NCH, k - 1))
                        cols = slice(k * P, (k + 1) * P)
                        weights5(UB[k % 2][:, :], UP0h[:, cols], UP0l[:, cols], UP1h[:, cols], UP1l[:, cols],
                                 Z0h[m.par][:, :], Z0l[m.par][:, :], Z1[m.par][:, :]).then_inc(s_up, 1)
                    if b is not None:
                        stage_b(b, k)
                    j, g = chunk_at(k, LAG, m, t)
                    if g is not None:
                        pe.wait_ge(s_ul, g.of(NCH, j + 1))
                        if j == 0 and t is not None:
                            pe.wait_ge(s_ot, g.of(2, 0))
                        for c in range(TR):
                            dst = two(AC[c // 2])[:, c % 2, :]
                            tok = slice(c * P, (c + 1) * P)
                            for n, (u, w) in enumerate(((Uh, DNh), (Uh, DNl), (Ul, DNh))):
                                last = pe.matmul(dst, u[j % 2][:, tok], w[:, j, :], start=j == 0 and n == 0 and c % 2 == 0,
                                                 stop=j == NCH - 1 and n == 2, skip_group_check=True)
                        last.then_inc(s_dn, 1)
                    if a is not None:
                        stage_a(a, k)

            schedule(pe, step)


_IN = ["x", "coords", "w_proj", "norm_w", "w_qk", "b_qk", "w_v", "b_v", "w_c", "b_c", "w_up", "w_down", "w_router", "b_bal"]


def kernel(**inputs):
    import numpy as np
    import concourse.bacc as bacc
    from concourse.bass_utils import run_bass_kernel_spmd

    a = {k.replace("L0_", ""): np.asarray(v) for k, v in inputs.items()}
    wq, wk = a["attn_Wq"].T, a["attn_Wk"].T
    bq, bk = a["attn_bq"], a["attn_bk"]
    up = np.concatenate([a["ffn_w1"].transpose(1, 0, 2).reshape(D, NE * D), a["ffn_w_fc_sh"]], axis=1)
    down = np.concatenate([a["ffn_w2"].reshape(NE * D, D), a["ffn_w_proj_sh"]], axis=0)
    laid = {
        "x": a["x"], "coords": a["tok_basin_coords"], "w_proj": a["tok_proj_w"].T, "norm_w": a["tok_norm_w"],
        "w_qk": np.concatenate([wq[:, :P], wk[:, :P], wq[:, P:], wk[:, P:]], axis=1),
        "b_qk": np.concatenate([bq[:P], bk[:P], bq[P:], bk[P:]]).reshape(3, P).T,
        "w_v": a["attn_Wv"].T, "b_v": a["attn_bv"], "w_c": a["attn_Wc"].T, "b_c": a["attn_bc"],
        "w_up": np.pad(up, ((0, 0), (0, HP - HID))), "w_down": np.pad(down, ((0, HP - HID), (0, 0))),
        "w_router": a["ffn_router_w"].T, "b_bal": a["ffn_balance_bias"],
    }
    nc = bacc.Bacc("TRN2", target_bir_lowering=False, num_devices=1)
    arrays, args = {}, []
    for name in _IN:
        v = np.ascontiguousarray(laid[name])
        arrays[f"in_{name}"] = v
        args.append(nc.dram_tensor(f"in_{name}", v.shape, mybir.dt.from_np(v.dtype), kind="ExternalInput").ap())
    args.append(nc.dram_tensor("out_y", (BATCH, SEQ, D), mybir.dt.float32, kind="ExternalOutput").ap())
    tower_kernel(nc, *args)
    r = run_bass_kernel_spmd(nc, [arrays], core_ids=[0])
    return r.results[0]["out_y"]
```

```python
import concourse.bass as bass
from concourse import mybir
from contextlib import ExitStack

P = 128
D = 192
KD = 64
DR = D - P
VOCAB = 32000
BATCH, SEQ = 16, 256
GT = 512
STEPS = BATCH * SEQ // GT
TR = GT // P
SG = GT // SEQ
QT = SEQ // P
NE = 8
HID = (NE + 1) * D
NCH = -(-HID // P)
ECH = NE * D // P
HP = NCH * P
LAG = 3
NU = 3
SCALE = float(D) ** -0.5
EPS_RMS, EPS_LN, EPS_TOP = 1e-8, 1e-5, 1e-20
BIG = 3.0e38


class Group:

    def __init__(self, i, off):
        self.n = 2 * i + off if off else 2 * i
        self.par = off % 2
        self.half = i + off // 2 if off // 2 else i

    def of(self, each, k):
        return self.n * each + k if k else self.n * each


def tower_kernel(nc, x, coords, w_proj, norm_w, w_qk, b_qk, w_v, b_v, w_c, b_c, w_up, w_down, w_router, b_bal, out):
    f32, f32r, i32 = mybir.dt.float32, mybir.dt.float32r, mybir.dt.int32
    ALU, ACT, AX = mybir.AluOpType, mybir.ActivationFunctionType, mybir.AxisListType

    ids_v = x.rearrange("b s -> (b s)").rearrange("(n p r) -> p n r", p=P, r=TR)
    out_v = out.rearrange("b s d -> (b s d)").rearrange("(n p f) -> n p f", p=P, f=TR * D)
    comb_dram = nc.dram_tensor("comb_scratch", (2, TR, NE, P), f32).ap()

    ctx = ExitStack()
    with ctx:
        def sb(name, shape, dt=f32):
            return ctx.enter_context(nc.sbuf_tensor(name, shape, dt))

        def sem(name):
            return ctx.enter_context(nc.semaphore(name))

        ident = sb("ident", [P, P])
        ones = sb("ones", [P, P], f32r)
        nhalf = sb("nhalf", [P, TR])
        phalf = sb("phalf", [P, 1])
        rank = sb("rank", [P, TR, NE])
        normw = sb("normw", [P, D])
        balb = sb("balb", [P, NE])
        bqk = sb("bqk", [P, 3])
        PJh, PJl = sb("PJh", [P, D], f32r), sb("PJl", [P, D], f32r)
        QK0h, QK0l, QK1h, QK1l = [sb(f"QK{s}", [P, 2 * D], f32r) for s in ("0h", "0l", "1h", "1l")]
        WV0h, WV0l, WV1h, WV1l = [sb(f"WV{s}", [P, D], f32r) for s in ("0h", "0l", "1h", "1l")]
        WCh, WCl = [sb(f"WC{s}", [P, 4, D], f32r) for s in ("h", "l")]
        RW0, RW1 = [sb(f"RW{s}", [P, 2, NE], f32r) for s in ("0", "1")]
        BVC = sb("BVC", [P, 2 * D], f32r)
        UP0h, UP0l, UP1h, UP1l = [sb(f"UP{s}", [P, HP], f32r) for s in ("0h", "0l", "1h", "1l")]
        DNh, DNl = [sb(f"DN{s}", [P, NCH, D], f32r) for s in ("h", "l")]
        ids = sb("ids", [P, STEPS, TR], i32)
        rows = sb("rows", [P, STEPS, TR], i32)
        row_now = [sb(f"row_now{i}", [P, TR], i32) for i in range(2)]
        G = [sb(f"G{i}", [P, TR, KD]) for i in range(2)]
        ss = sb("ss", [P, TR])
        Fw = [sb(f"Fw{i}", [P, TR, D]) for i in range(2)]
        st = sb("st", [P, TR, 6])
        idf, neg = [Fw[0][:, i, 0:STEPS * TR].rearrange("p (n r) -> p n r", r=TR) for i in range(2)]
        mm = sb("mm", [P, 6, TR])
        sA = sb("sA", [P, 4, TR])
        sr1 = [sb(f"sr1{i}", [P, TR]) for i in range(2)]
        sscl = sb("sscl", [P, TR])
        X0h, X0l, X1 = [sb(f"X{s}", [P, GT], f32r) for s in ("0h", "0l", "1")]
        QB, KB = sb("QB", [P, 2, GT], f32r), sb("KB", [P, 2, GT], f32r)
        Q0h, Q0l, K0h, K0l = QB[:, 0, :], QB[:, 1, :], KB[:, 0, :], KB[:, 1, :]
        Q1 = sb("Q1", [P, GT], f32r)
        GTs = Q1
        K1h, K1l = sb("K1h", [P, GT], f32r), sb("K1l", [P, GT], f32r)
        Vh, Vl = [sb(f"V{s}", [P, TR, D], f32r) for s in ("h", "l")]
        mx = sb("mx", [P, SG, QT])
        nb = sb("nb", [P, SG, QT])
        rs = sb("rs", [P, SG, QT])
        ri = sb("ri", [P, SG, QT])
        Pr = sb("Pr", [P, SG, QT, SEQ])
        xn = Pr[:, :, :, :].rearrange("p a b c -> p (a b c)")[:, 0:TR * D].rearrange("p (c w) -> p c w", c=2)
        Yh, Yl = [t[:, :, :].rearrange("p a b -> p (a b)")[:, 0:TR * D]
                  .rearrange("p (q c s a) -> p q c s a", q=QT, c=3, s=SG) for t in (QB, KB)]
        PTh, PTl = [sb(f"PT{s}", [P, SG, QT, SEQ], f32r) for s in ("h", "l")]
        h2 = [sb(f"h2{i}", [P, TR, D]) for i in range(2)]
        st2 = sb("st2", [P, TR, 6])
        mm2 = sb("mm2", [P, 6, TR])
        ve2 = sb("ve2", [P, TR])
        s2 = sb("s2", [P, TR])
        Z0h, Z0l, Z1 = [[sb(f"Z{s}_{i}", [P, GT], f32r) for i in range(2)] for s in ("0h", "0l", "1")]
        rt = sb("rt", [P, 14, TR, NE])
        rm = sb("rm", [P, 12, TR])
        combT = sb("combT", [P, P])
        combB = [sb(f"combB{i}", [P, ECH, GT]) for i in range(2)]
        OUT = [t[:, :, :].rearrange("p a b -> p (a b)")[:, 0:TR * D] for t in combB]
        R = [sb(f"R{i}", [P, GT]) for i in range(2)]
        U = [sb(f"U{i}", [P, GT]) for i in range(2)]
        Uh, Ul = [[sb(f"U{s}{i}", [P, GT], f32r) for i in range(NU)] for s in ("h", "l")]
        raw0 = combB[0][:, :, :].rearrange("p a b -> p (a b)")
        raw1 = combB[1][:, :, :].rearrange("p a b -> p (a b)")
        at = [0]

        def raw(base, n):
            at[0] += n
            assert at[0] <= ECH * GT
            return base[:, at[0] - n:at[0]]
        rPJ = raw(raw0, D)
        rQK0, rQK1 = raw(raw0, 2 * D), raw(raw0, 2 * D)
        rWV0, rWV1 = raw(raw0, D), raw(raw0, D)
        rWC = raw(raw0, 4 * D)
        rRW0, rRW1 = raw(raw0, NE), raw(raw0, NE)
        rB = raw(raw0, 2 * D)
        rDN = raw(raw0, NCH * D)
        at[0] = 0
        rUP0, rUP1 = raw(raw1, HP), raw(raw1, HP)

        def bank(name):
            return ctx.enter_context(nc.psum_tensor(name, [P, 512], f32))
        A = [bank("A0"), bank("A1")]
        B = [bank("B0"), bank("B1")]
        UB = [bank("U0p"), bank("U1p")]
        AC = [bank("acc0"), bank("acc1")]

        def two(t):
            return t[:, 0:2 * D].rearrange("p (a d) -> p a d", a=2)

        def halves(t):
            return t[:, 0:2 * P].rearrange("q (c p) -> q c p", c=2)

        def pair(t):
            return t[:, :].rearrange("q (c o p) -> q o c p", c=2, o=2)

        def pair_tok(t):
            return t[:, :].rearrange("q (p c o) -> q o c p", c=2, o=2)

        s_raw = [sem(f"raw_loaded{i}") for i in range(4)]
        s_zero = sem("stage_zeroed")
        s_const = sem("constants_made")
        s_ones = sem("ones_made")
        s_ids = sem("ids_loaded")
        s_rows = sem("rows_clamped")
        s_whi = sem("weight_hi_made")
        s_wlo = sem("weight_lo_made")
        s_gath = [sem(f"gathered{i}") for i in range(2)]
        s_rowc = sem("row_numbers_copied")
        s_gt = sem("pe_basin_transposed")
        s_gth = sem("basin_hi_made")
        s_gtl = sem("basin_lo_made")
        s_e = sem("pe_embedded")
        s_sq = sem("squares_summed")
        s_fw = sem("embedding_weighted")
        s_st = sem("stats_made")
        s_mv = sem("moments_made")
        s_ps = sem("pool_scale_steps")
        s_xn = sem("normed")
        s_xt = sem("pe_normed_transposed")
        s_xh = sem("normed_hi_made")
        s_xl = sem("normed_lo_made")
        s_qk = sem("pe_qk_made")
        s_qkh = sem("qk_hi_made")
        s_qkl = sem("qk_lo_made")
        s_v = sem("pe_v_made")
        s_vh = sem("v_hi_made")
        s_vl = sem("v_lo_made")
        s_s = sem("pe_scores_made")
        s_mx = sem("row_max_found")
        s_nb = sem("exp_bias_made")
        s_ex = sem("exps_made")
        s_ri = sem("row_sums_inverted")
        s_pt = sem("pe_probabilities_transposed")
        s_pth = sem("probability_hi_made")
        s_ptl = sem("probability_lo_made")
        s_y = sem("pe_attended")
        s_yh = sem("attended_hi_made")
        s_yl = sem("attended_lo_made")
        s_wc = sem("pe_attention_out_made")
        s_h2 = sem("second_residual_made")
        s_st2 = sem("second_stats_made")
        s_mv2 = sem("second_moments_made")
        s_p2 = sem("pool_second_scale_steps")
        s_xn2 = sem("second_normed")
        s_zt = sem("pe_second_normed_transposed")
        s_zh = sem("second_normed_hi_made")
        s_zl = sem("second_normed_lo_made")
        s_rt = sem("pe_logits_made")
        s_lg = sem("logit_halves_added")
        s_re = sem("logit_exps_made")
        s_rc = sem("router_steps")
        s_comb = sem("shares_made")
        s_root = sem("root_steps")
        s_ct = sem("pe_combine_transposed")
        s_cs = sem("combine_copied")
        s_cd = sem("combine_stored")
        s_cb = [[sem(f"combine_spread{i}_{g}") for g in range(NE // 2)] for i in range(2)]
        s_up = sem("pe_up_made")
        s_r = sem("relu_made")
        s_t = sem("hidden_weighted")
        s_u = sem("hidden_squared")
        s_uh = sem("hidden_hi_made")
        s_ul = sem("hidden_lo_made")
        s_dn = sem("pe_down_made")
        s_ot = sem("output_made")
        s_out = sem("output_stored")
        NRC = 18

        GT_, E_, RMS_, BN_, XN_, XT_, QK_, V_, S_, EXP_, PT_ = 0, 1, 2, 3, 4, 5, (6, 7, 8), (9, 12), (9, 10), (10, 11), (11, 12)
        Y_, WC_, XN2_, ZT_, RT_, ROUTE_, ROOT_, CT_ = (0, 1), 2, 3, 4, 5, (5, 6, 7), 8, 9
        GATHER_ = (5, 7, 10, 12)

        block = ctx.enter_context(nc.Block())

        def schedule(eng, step):
            step(Group(0, 0), None, None, None)
            step(Group(0, 1), Group(0, 0), None, None)
            step(Group(0, 2), Group(0, 1), Group(0, 0), None)
            step(Group(0, 3), Group(0, 2), Group(0, 1), Group(0, 0))
            with eng.Fori(1, STEPS // 2 - 1) as i:
                step(Group(i, 2), Group(i, 1), Group(i, 0), Group(i, -1))
                step(Group(i, 3), Group(i, 2), Group(i, 1), Group(i, 0))
            last = STEPS // 2 - 1
            step(None, Group(last, 1), Group(last, 0), Group(last, -1))
            step(None, None, Group(last, 1), Group(last, 0))
            step(None, None, None, Group(last, 1))

        def chunk_at(k, lag, m, t):
            return (k - lag, m) if k >= lag else (k - lag + NCH, t)

        def downs_at(k, m, t):
            late = {0: (ECH - 1, ECH), 1: (ECH + 1,)}
            at = [(k - LAG, m)] if k >= LAG else [(j, t) for j in late.get(k, ())]
            return [(j, g) for j, g in at if g is not None]

        @block.sync
        def _(sp):
            sp.dma_start(ids[:, :, :], ids_v).then_inc(s_ids, 16)
            for half in (0, KD):
                sp.dma_start(rPJ[half:half + KD, :], w_proj).then_inc(s_raw[0], 16)
            sp.dma_start(normw[:, :], norm_w.partition_broadcast(P)).then_inc(s_raw[0], 16)
            sp.dma_start(rQK0, w_qk[0:P, :]).then_inc(s_raw[1], 16)
            for half in (0, KD):
                sp.dma_start(rQK1[half:half + DR, :], w_qk[P:D, :]).then_inc(s_raw[1], 16)
            sp.dma_start(bqk[:, :], b_qk).then_inc(s_raw[1], 16)
            sp.dma_start(rWV0, w_v[0:P, :]).then_inc(s_raw[2], 16)
            sp.dma_start(rRW0, w_router[0:P, :]).then_inc(s_raw[2], 16)
            for half in (0, KD):
                sp.dma_start(rWV1[half:half + DR, :], w_v[P:D, :]).then_inc(s_raw[2], 16)
                sp.dma_start(rRW1[half:half + DR, :], w_router[P:D, :]).then_inc(s_raw[2], 16)
            sp.dma_start(balb[:, :], b_bal.partition_broadcast(P)).then_inc(s_raw[2], 16)
            sp.wait_ge(s_zero, 2)
            sp.dma_start(rWC[:, 0:D], w_c[0:P, :]).then_inc(s_raw[2], 16)
            sp.dma_start(rWC[:, D:2 * D], w_c[KD:KD + P, :]).then_inc(s_raw[2], 16)
            sp.dma_start(rWC[0:KD, 2 * D:3 * D], w_c[P:D, :]).then_inc(s_raw[2], 16)
            sp.dma_start(rWC[KD:P, 3 * D:4 * D], w_c[0:KD, :]).then_inc(s_raw[2], 16)
            for row in (0, 32):
                sp.dma_start(rB[row:row + 1, 0:D], b_v.rearrange("(a n) -> a n", a=1)).then_inc(s_raw[2], 16)
                sp.dma_start(rB[row:row + 1, D:2 * D], b_c.rearrange("(a n) -> a n", a=1)).then_inc(s_raw[2], 16)
            sp.dma_start(rUP0, w_up[0:P, :]).then_inc(s_raw[3], 16)
            for half in (0, KD):
                sp.dma_start(rUP1[half:half + DR, :], w_up[P:D, :]).then_inc(s_raw[3], 16)
            sp.dma_start(rDN.rearrange("p (c n) -> p c n", c=NCH),
                         w_down.rearrange("(c p) n -> p c n", p=P)).then_inc(s_raw[3], 16)

            def step(a, b, m, t):
                if t is not None:
                    sp.wait_ge(s_ot, t.of(2, 2))
                    sp.dma_start(out_v[t.n, :, :], OUT[t.par]).then_inc(s_out, 16)
                if b is not None:
                    sp.wait_ge(s_cs, b.of(1, 1))
                    sp.dma_start(comb_dram[b.par].rearrange("r e p -> (r e) p"), combT[P - TR * NE:P, :]).then_inc(s_cd, 16)
                    sp.wait_ge(s_cd, b.of(16, 16))
                    if t is not None:
                        sp.wait_ge(s_out, t.of(16, 16))
                    for g in range(NE // 2):
                        for lo, hi, j, odd in ((0, P, 0, 0), (0, KD, 1, 0), (KD, P, 1, 1), (0, P, 2, 1)):
                            sp.dma_start(combB[b.par][lo:hi, 3 * g + j, :].rearrange("q (r p) -> q r p", r=TR),
                                         comb_dram[b.par, :, 2 * g + odd, :].partition_broadcast(hi - lo))\
                              .then_inc(s_cb[b.par][g], 16)

            schedule(sp, step)
            sp.wait_ge(s_out, 16 * STEPS)

        @block.gpsimd
        def _(pool):
            pool.memset(rWC, 0.0).then_inc(s_zero, 1)
            pool.memset(rB, 0.0).then_inc(s_zero, 1)
            pool.memset(ident[:, :], 0.0).then_inc(s_const, 1)
            pool.wait_ge(s_const, 1)
            pool.affine_select(out=ident[:, :], in_=ident[:, :], compare_op=ALU.not_equal, fill=1.0, base=0,
                               pattern=[[-1, P]], channel_multiplier=1).then_inc(s_const, 1)
            pool.memset(nhalf[:, :], -0.5).then_inc(s_const, 1)
            pool.memset(phalf[:, :], 0.5).then_inc(s_const, 1)
            for e in range(NE):
                pool.memset(rank[:, :, e:e + 1], float(NE - e)).then_inc(s_const, 1)

            def gather(g, r):
                if r == 0:
                    pool.tensor_copy(row_now[g.par][:, :], rows[:, g.n, :]).then_inc(s_rowc, 1)
                    pool.wait_ge(s_rowc, g.of(1, 1))
                    if not (isinstance(g.n, int) and g.n < 2):
                        pool.wait_ge(s_gt, g.of(1, -1))
                pool.indirect_dma_start(out=G[g.par][:, r, :], out_offset=None, in_=coords,
                                        in_offset=bass.IndirectOffsetOnAxis(ap=row_now[g.par][:, r:r + 1], axis=0))\
                    .then_inc(s_gath[g.par], 16)

            pool.wait_ge(s_const, 12)
            pool.wait_ge(s_rows, 5)
            for r in range(TR):
                gather(Group(0, 0), r)

            def step(a, b, m, t, following):
                for k in range(NCH):
                    if a is not None and k == RMS_:
                        pool.wait_ge(s_sq, a.of(2, 2))
                        pool.tensor_scalar(sA[:, 0, :], ss[:, :], 1.0 / D, EPS_RMS, ALU.mult, ALU.add).then_inc(s_ps, 1)
                        pool.wait_ge(s_ps, a.of(7, 1))
                        pool.tensor_tensor(sr1[a.par][:, :], sA[:, 0, :], nhalf[:, :], ALU.pow).then_inc(s_ps, 1)
                        pool.wait_ge(s_ps, a.of(7, 2))
                        pool.tensor_tensor(sA[:, 1, :], sr1[a.par][:, :], sr1[a.par][:, :], ALU.mult).then_inc(s_ps, 1)
                        pool.wait_ge(s_ps, a.of(7, 3))
                    if a is not None and k == XN_:
                        pool.wait_ge(s_mv, a.of(3, 3))
                        pool.tensor_tensor(sA[:, 2, :], sA[:, 1, :], mm[:, 5, :], ALU.mult).then_inc(s_ps, 1)
                        pool.wait_ge(s_ps, a.of(7, 4))
                        pool.tensor_scalar(sA[:, 3, :], sA[:, 2, :], 1.0 / D, EPS_LN, ALU.mult, ALU.add).then_inc(s_ps, 1)
                        pool.wait_ge(s_ps, a.of(7, 5))
                        pool.tensor_tensor(sA[:, 0, :], sA[:, 3, :], nhalf[:, :], ALU.pow).then_inc(s_ps, 1)
                        pool.wait_ge(s_ps, a.of(7, 6))
                        pool.tensor_tensor(sscl[:, :], sA[:, 0, :], sr1[a.par][:, :], ALU.mult).then_inc(s_ps, 1)
                    if b is not None and k == XN2_:
                        pool.wait_ge(s_mv2, b.of(3, 3))
                        pool.tensor_scalar(ve2[:, :], mm2[:, 5, :], 1.0 / D, EPS_LN, ALU.mult, ALU.add).then_inc(s_p2, 1)
                        pool.wait_ge(s_p2, b.of(2, 1))
                        pool.tensor_tensor(s2[:, :], ve2[:, :], nhalf[:, :], ALU.pow).then_inc(s_p2, 1)
                    if b is not None and k == ROOT_:
                        pool.wait_ge(s_comb, b.of(1, 1))
                        pool.tensor_tensor(rm[:, 10:12, :], rm[:, 8:10, :],
                                           phalf[:, 0:1].unsqueeze(2).to_broadcast([P, 2, TR]), ALU.pow).then_inc(s_root, 1)
                        pool.wait_ge(s_root, b.of(3, 1))
                        pool.tensor_tensor(rt[:, 11:13, :, :], rt[:, 6:11:4, :, :],
                                           rm[:, 10:12, :].unsqueeze(3).to_broadcast([P, 2, TR, NE]), ALU.mult).then_inc(s_root, 1)
                        pool.wait_ge(s_root, b.of(3, 2))
                        pool.tensor_tensor(rt[:, 13, :, :], rt[:, 11, :, :], rt[:, 12, :, :], ALU.add).then_inc(s_root, 1)
                    if m is not None and k < ECH:
                        if k % 3 == 0:
                            pool.wait_ge(s_cb[m.par][k // 3], m.half * 64 + 64)
                        pool.wait_ge(s_r, m.of(NCH, k + 1))
                        if t is not None or k >= 2:
                            pool.wait_ge(s_ul, m.of(NCH, k - 1))
                        pool.tensor_tensor(U[k % 2][:, :], R[k % 2][:, :], combB[m.par][:, k, :], ALU.mult)\
                            .then_inc(s_t, 1)
                    if following is not None and k in GATHER_:
                        gather(following, GATHER_.index(k))

            step(Group(0, 0), None, None, None, Group(0, 1))
            step(Group(0, 1), Group(0, 0), None, None, Group(0, 2))
            step(Group(0, 2), Group(0, 1), Group(0, 0), None, Group(0, 3))
            step(Group(0, 3), Group(0, 2), Group(0, 1), Group(0, 0), Group(0, 4))
            with pool.Fori(1, STEPS // 2 - 2) as i:
                step(Group(i, 2), Group(i, 1), Group(i, 0), Group(i, -1), Group(i, 3))
                step(Group(i, 3), Group(i, 2), Group(i, 1), Group(i, 0), Group(i, 4))
            i = STEPS // 2 - 2
            step(Group(i, 2), Group(i, 1), Group(i, 0), Group(i, -1), Group(i, 3))
            step(Group(i, 3), Group(i, 2), Group(i, 1), Group(i, 0), None)
            last = STEPS // 2 - 1
            step(None, Group(last, 1), Group(last, 0), Group(last, -1), None)
            step(None, None, Group(last, 1), Group(last, 0), None)

        def pieces(rawt, hi, lo, n, w=GT):
            return [(rawt[:, c:min(c + w, n)], hi[:, c:min(c + w, n)], lo[:, c:min(c + w, n)]) for c in range(0, n, w)]

        flatC = [t[:, :, :].rearrange("p a b -> p (a b)") for t in (WCh, WCl)]
        flatD = [t[:, :, :].rearrange("p a b -> p (a b)") for t in (DNh, DNl)]
        proj_w = pieces(rPJ, PJh, PJl, D)
        qk_w = pieces(rQK0, QK0h, QK0l, 2 * D) + pieces(rQK1, QK1h, QK1l, 2 * D)
        rest_w = (pieces(rWV0, WV0h, WV0l, D) + pieces(rWV1, WV1h, WV1l, D) +
                  pieces(rWC, flatC[0], flatC[1], 4 * D, 4 * D) +
                  [(r, w[:, 0, :], w[:, 1, :]) for r, w in ((rRW0, RW0), (rRW1, RW1))])
        mlp_w = pieces(rUP0, UP0h, UP0l, HP) + pieces(rUP1, UP1h, UP1l, HP) + pieces(rDN, flatD[0], flatD[1], NCH * D)
        QK_LOADS, REST_LOADS, MLP_LOADS = 4, 15, 4
        QKW_, RESTW_, MLPW_ = 4, 6, 7
        N_PROJ = len(proj_w)
        N_QK = N_PROJ + len(qk_w)
        N_REST = N_QK + len(rest_w) + 1
        N_ALL = N_REST + len(mlp_w)

        def mlp_split_at(k):
            slots, n = NCH - MLPW_, k - MLPW_
            lo, hi = [x * len(mlp_w) // slots for x in (n, n + 1)]
            return [(N_REST + x, mlp_w[x]) for x in range(lo, hi)] if k >= MLPW_ else []

        @block.scalar
        def _(act):
            act.preload_act_table(ACT.Exp)
            act.wait_ge(s_raw[0], 48)
            for src, hi, lo in proj_w:
                act.activation(hi, src, ACT.Copy).then_inc(s_whi, 1)

            def split(k):
                if k == QKW_:
                    act.wait_ge(s_raw[1], 16 * QK_LOADS)
                    for src, hi, lo in qk_w:
                        act.activation(hi, src, ACT.Copy).then_inc(s_whi, 1)
                if k == RESTW_:
                    act.wait_ge(s_raw[2], 16 * REST_LOADS)
                    for src, hi, lo in rest_w:
                        act.activation(hi, src, ACT.Copy).then_inc(s_whi, 1)
                    act.activation(BVC[:, :], rB, ACT.Copy).then_inc(s_whi, 1)
                if k == MLPW_:
                    act.wait_ge(s_raw[3], 16 * MLP_LOADS)
                for n, (src, hi, lo) in mlp_split_at(k):
                    act.activation(hi, src, ACT.Copy).then_inc(s_whi, 1)

            def step(a, b, m, t):
                for k in range(NCH):
                    if a is not None and b is None:
                        split(k)
                    j, g = chunk_at(k, 1, m, t)
                    if g is not None:
                        if j < ECH:
                            act.wait_ge(s_t, g.of(ECH, j + 1))
                            act.activation(U[j % 2][:, :], U[j % 2][:, :], ACT.Square).then_inc(s_u, 1)
                        else:
                            act.wait_ge(s_r, g.of(NCH, j + 1))
                            act.wait_ge(s_ul, g.of(NCH, j - 1))
                            act.activation(U[j % 2][:, :], R[j % 2][:, :], ACT.Square).then_inc(s_u, 1)
                    if a is not None:
                        if k == GT_:
                            act.wait_ge(s_gt, a.of(1, 1))
                            for o in range(2):
                                last = act.activation(pair(GTs)[0:KD, o], halves(A[0])[o * KD:(o + 1) * KD], ACT.Copy)
                            last.then_inc(s_gth, 1)
                        if k == E_:
                            for c in range(2):
                                act.wait_ge(s_e, a.of(2, c + 1))
                                for r in range(2):
                                    last = act.activation(Fw[a.par][:, 2 * c + r, :], A[1 - c][:, r * D:(r + 1) * D], ACT.Square,
                                                          accum_out=ss[:, 2 * c + r:2 * c + r + 1])
                                last.then_inc(s_sq, 1)
                        if k == XT_:
                            act.wait_ge(s_xt, a.of(2, 1))
                            act.activation(X0h[:, :].rearrange("q (p r) -> q p r", r=TR),
                                           A[1][:, :].rearrange("q (r p) -> q p r", r=TR), ACT.Copy).then_inc(s_xh, 1)
                            act.wait_ge(s_xt, a.of(2, 2))
                            for o in range(2):
                                last = act.activation(pair_tok(X1)[0:DR, o], halves(A[0])[o * DR:(o + 1) * DR], ACT.Copy)
                            last.then_inc(s_xh, 1)
                        if k == QK_[0]:
                            act.wait_ge(s_qk, a.of(3, 1))
                            act.activation(Q0h[:, :], A[1][:, :], ACT.Identity, bias=bqk[:, 0:1]).then_inc(s_qkh, 1)
                        if k == QK_[1]:
                            act.wait_ge(s_qk, a.of(3, 2))
                            act.activation(K0h[:, :], A[0][:, :], ACT.Identity, bias=bqk[:, 1:2]).then_inc(s_qkh, 1)
                        if k == QK_[2]:
                            act.wait_ge(s_qk, a.of(3, 3))
                            act.activation(K1h[0:KD, :], A[1][KD:P, :], ACT.Identity, bias=bqk[KD:P, 2:3])
                            act.activation(K1h[KD:P, :], A[1][KD:P, :], ACT.Identity, bias=bqk[KD:P, 2:3])
                            act.activation(Q1[0:KD, :], A[1][0:KD, :], ACT.Identity, bias=bqk[0:KD, 2:3])\
                               .then_inc(s_qkh, 1)
                        for c in range(2):
                            if k == V_[c]:
                                act.wait_ge(s_v, a.of(2, c + 1))
                                act.activation(Vh[:, 2 * c:2 * c + 2, :], two(A[c]), ACT.Copy).then_inc(s_vh, 1)
                            if k == EXP_[c]:
                                act.wait_ge(s_nb, a.of(2, c + 1))
                                for q in range(QT):
                                    last = act.activation(Pr[:, c, q, :], B[c][:, q * SEQ:(q + 1) * SEQ], ACT.Exp,
                                                          bias=nb[:, c, q:q + 1], scale=SCALE,
                                                          accum_out=rs[:, c, q:q + 1])
                                last.then_inc(s_ex, 1)
                            if k == PT_[c]:
                                act.wait_ge(s_pt, a.of(2, c + 1))
                                act.activation(PTh[:, c, :, :], B[c][:, :].rearrange("p (t q) -> p t q", t=QT), ACT.Copy)\
                                   .then_inc(s_pth, 1)
                    if b is not None:
                        for c in range(2):
                            if k == Y_[c]:
                                act.wait_ge(s_y, b.of(2, c + 1))
                                act.wait_ge(s_ri, b.of(2, c + 1))
                                for q in range(QT):
                                    last = act.activation(Yh[:, q, :, c, :],
                                                          two(B[c])[:, q, :].rearrange("p (a c) -> p c a", c=3),
                                                          ACT.Identity, scale=ri[:, c, q:q + 1])
                                last.then_inc(s_yh, 1)
                        if k == ZT_:
                            act.wait_ge(s_zt, b.of(2, 1))
                            act.activation(Z0h[b.par][:, :], B[0][:, :], ACT.Copy).then_inc(s_zh, 1)
                            act.wait_ge(s_zt, b.of(2, 2))
                            for o in range(2):
                                last = act.activation(pair(Z1[b.par])[0:DR, o], halves(B[1])[o * DR:(o + 1) * DR], ACT.Copy)
                            last.then_inc(s_zh, 1)
                        if k == RT_:
                            act.wait_ge(s_lg, b.of(1, 1))
                            act.activation(rt[:, 0, :, :], rt[:, 13, :, :], ACT.Exp, scale=-1.0).then_inc(s_re, 1)
                        if k == CT_:
                            act.wait_ge(s_ct, b.of(1, 1))
                            if not (isinstance(b.n, int) and b.n == 0):
                                act.wait_ge(s_cd, b.of(16, 0))
                            act.activation(combT[P - TR * NE:P, :], B[1][P - TR * NE:P, 0:P], ACT.Copy).then_inc(s_cs, 1)
                    if g is not None:
                        act.wait_ge(s_u, g.of(NCH, j + 1))
                        if j >= NU:
                            act.wait_ge(s_dn, g.of(NCH, j - NU + 1))
                        elif not (isinstance(g.n, int) and g.n == 0):
                            act.wait_ge(s_dn, g.of(NCH, (-1, 0, -2)[j]))
                        act.activation(Uh[j % NU][:, :], U[j % 2][:, :], ACT.Copy).then_inc(s_uh, 1)
                    if m is not None:
                        act.wait_ge(s_up, m.of(NCH, k + 1))
                        if t is not None or k >= 2:
                            act.wait_ge(s_u, m.of(NCH, k - 1))
                        act.activation(R[k % 2][:, :], UB[k % 2][:, :], ACT.Relu).then_inc(s_r, 1)

            schedule(act, step)

        @block.vector
        def _(dve):
            dve.memset(ones[:, :].bitcast(f32), 1.0).then_inc(s_ones, 1)
            dve.memset(K1l[KD:P, :].bitcast(f32), 0.0).then_inc(s_ones, 1)
            dve.wait_ge(s_ids, 16)
            dve.tensor_copy(idf[:, :, :], ids[:, :, :]).then_inc(s_rows, 1)
            dve.wait_ge(s_rows, 1)
            dve.tensor_scalar(neg[:, :, :], idf[:, :, :], 0.0, float(VOCAB), ALU.is_lt, ALU.mult).then_inc(s_rows, 1)
            dve.wait_ge(s_rows, 2)
            dve.tensor_tensor(neg[:, :, :], idf[:, :, :], neg[:, :, :], ALU.add).then_inc(s_rows, 1)
            dve.wait_ge(s_rows, 3)
            dve.tensor_scalar(idf[:, :, :], neg[:, :, :], 0.0, float(VOCAB - 1), ALU.max, ALU.min).then_inc(s_rows, 1)
            dve.wait_ge(s_rows, 4)
            dve.tensor_copy(rows[:, :, :], idf[:, :, :]).then_inc(s_rows, 1)

            def lows(made, pieces):
                for n, (src, hi, lo) in enumerate(pieces):
                    dve.wait_ge(s_whi, made + n + 1)
                    dve.tensor_tensor(lo, src, hi.bitcast(f32), ALU.subtract).then_inc(s_wlo, 1)

            lows(0, proj_w)

            def split(k):
                if k == QKW_:
                    lows(N_PROJ, qk_w)
                if k == RESTW_:
                    lows(N_QK, rest_w)
                    dve.wait_ge(s_whi, N_REST)
                    dve.tensor_tensor(BVC[32:33, :], rB[32:33, :], BVC[32:33, :].bitcast(f32), ALU.subtract).then_inc(s_wlo, 1)
                for n, piece in mlp_split_at(k):
                    lows(n, [piece])

            def step(a, b, m, t):
                for k in range(NCH):
                    if a is not None and b is None:
                        split(k)
                    if t is not None and k == WC_:
                        dve.wait_ge(s_dn, t.of(NCH, NCH))
                        for c in range(2):
                            dve.tensor_tensor(OUT[t.par][:, 2 * c * D:(2 * c + 2) * D].rearrange("p (r d) -> p r d", r=2), two(AC[c]),
                                              h2[t.par][:, 2 * c:2 * c + 2, :], ALU.add).then_inc(s_ot, 1)
                    if a is not None:
                        if k == GT_:
                            dve.wait_ge(s_gth, a.of(1, 1))
                            for o in range(2):
                                last = dve.tensor_tensor(pair(GTs)[KD:P, o], halves(A[0])[o * KD:(o + 1) * KD],
                                                         pair(GTs)[0:KD, o].bitcast(f32), ALU.subtract)
                            last.then_inc(s_gtl, 1)
                        if k == E_:
                            for c in range(2):
                                dve.wait_ge(s_sq, a.of(2, c + 1))
                                dve.tensor_tensor(Fw[a.par][:, 2 * c:2 * c + 2, :], two(A[1 - c]),
                                                  normw[:, :].unsqueeze(1).to_broadcast([P, 2, D]), ALU.mult).then_inc(s_fw, 1)
                        if k == XT_:
                            dve.wait_ge(s_xh, a.of(2, 1))
                            dve.tensor_tensor(X0l[:, :].rearrange("q (p r) -> q p r", r=TR),
                                              A[1][:, :].rearrange("q (r p) -> q p r", r=TR),
                                              X0h[:, :].bitcast(f32).rearrange("q (p r) -> q p r", r=TR),
                                              ALU.subtract).then_inc(s_xl, 1)
                            dve.wait_ge(s_xh, a.of(2, 2))
                            for o in range(2):
                                last = dve.tensor_tensor(pair_tok(X1)[DR:P, o], halves(A[0])[o * DR:(o + 1) * DR],
                                                         pair_tok(X1)[0:DR, o].bitcast(f32), ALU.subtract)
                            last.then_inc(s_xl, 1)
                        if k == QK_[0]:
                            dve.wait_ge(s_qkh, a.of(3, 1))
                            dve.scalar_tensor_tensor(Q0l[:, :], A[1][:, :], bqk[:, 0:1], Q0h[:, :].bitcast(f32),
                                                     ALU.add, ALU.subtract).then_inc(s_qkl, 1)
                        if k == QK_[1]:
                            dve.wait_ge(s_qkh, a.of(3, 2))
                            dve.scalar_tensor_tensor(K0l[:, :], A[0][:, :], bqk[:, 1:2], K0h[:, :].bitcast(f32),
                                                     ALU.add, ALU.subtract).then_inc(s_qkl, 1)
                        if k == QK_[2]:
                            dve.wait_ge(s_qkh, a.of(3, 3))
                            dve.scalar_tensor_tensor(K1l[0:KD, :], A[1][KD:P, :], bqk[KD:P, 2:3],
                                                     K1h[KD:P, :].bitcast(f32), ALU.add, ALU.subtract)
                            dve.scalar_tensor_tensor(Q1[KD:P, :], A[1][0:KD, :], bqk[0:KD, 2:3],
                                                     Q1[0:KD, :].bitcast(f32), ALU.add, ALU.subtract).then_inc(s_qkl, 1)
                        for c in range(2):
                            if k == V_[c]:
                                dve.wait_ge(s_vh, a.of(2, c + 1))
                                dve.tensor_tensor(Vl[:, 2 * c:2 * c + 2, :], two(A[c]),
                                                  Vh[:, 2 * c:2 * c + 2, :].bitcast(f32), ALU.subtract).then_inc(s_vl, 1)
                            if k == PT_[c]:
                                dve.wait_ge(s_pth, a.of(2, c + 1))
                                dve.tensor_tensor(PTl[:, c, :, :], B[c][:, :].rearrange("p (t q) -> p t q", t=QT),
                                                  PTh[:, c, :, :].bitcast(f32), ALU.subtract).then_inc(s_ptl, 1)
                    if b is not None:
                        for c in range(2):
                            if k == Y_[c]:
                                dve.wait_ge(s_yh, b.of(2, c + 1))
                                for q in range(QT):
                                    last = dve.scalar_tensor_tensor(Yl[:, q, :, c, :],
                                                                    two(B[c])[:, q, :].rearrange("p (a c) -> p c a", c=3),
                                                                    ri[:, c, q:q + 1], Yh[:, q, :, c, :].bitcast(f32),
                                                                    ALU.mult, ALU.subtract)
                                last.then_inc(s_yl, 1)
                        if k == WC_:
                            if t is not None:
                                dve.wait_ge(s_ot, t.of(2, 2))
                            for c in range(2):
                                dve.wait_ge(s_wc, b.of(2, c + 1))
                                for r in (2 * c, 2 * c + 1):
                                    last = dve.scalar_tensor_tensor(h2[b.par][:, r, :], Fw[b.par][:, r, :], sr1[b.par][:, r:r + 1],
                                                                    two(B[c])[:, r % 2, :], ALU.mult, ALU.add)
                                last.then_inc(s_h2, 1)
                                dve.wait_ge(s_h2, b.of(2, c + 1))
                                for r in (2 * c, 2 * c + 1):
                                    last = dve.bn_stats(st2[:, r, :], h2[b.par][:, r, :])
                            last.then_inc(s_st2, 1)
                            moments(b, st2, mm2, s_st2, s_mv2)
                        if k == RT_:
                            dve.wait_ge(s_rt, b.of(1, 1))
                            dve.tensor_reduce(rt[:, 13, :, :], B[0][:, 0:2 * TR * NE].rearrange("p (r a e) -> p r e a", r=TR, a=2),
                                              AX.X, ALU.add).then_inc(s_lg, 1)
                        if k == ZT_:
                            dve.wait_ge(s_zh, b.of(2, 1))
                            dve.tensor_tensor(Z0l[b.par][:, :], B[0][:, :], Z0h[b.par][:, :].bitcast(f32), ALU.subtract)\
                               .then_inc(s_zl, 1)
                            dve.wait_ge(s_zh, b.of(2, 2))
                            for o in range(2):
                                last = dve.tensor_tensor(pair(Z1[b.par])[DR:P, o], halves(B[1])[o * DR:(o + 1) * DR],
                                                         pair(Z1[b.par])[0:DR, o].bitcast(f32), ALU.subtract)
                            last.then_inc(s_zl, 1)
                    if b is not None:
                        if k == XN2_:
                            dve.wait_ge(s_p2, b.of(2, 2))
                            normed(h2[b.par], mm2[:, 3, :], s2).then_inc(s_xn2, 1)
                    j, g = chunk_at(k, 1, m, t)
                    if g is not None:
                        dve.wait_ge(s_uh, g.of(NCH, j + 1))
                        dve.tensor_tensor(Ul[j % NU][:, :], U[j % 2][:, :], Uh[j % NU][:, :].bitcast(f32), ALU.subtract)\
                           .then_inc(s_ul, 1)
                    if b is not None:
                        if k in ROUTE_:
                            route(b, ROUTE_.index(k))
                    if a is not None:
                        if k == BN_:
                            dve.wait_ge(s_fw, a.of(2, 2))
                            for r in range(TR):
                                last = dve.bn_stats(st[:, r, :], Fw[a.par][:, r, :])
                            last.then_inc(s_st, 1)
                            moments(a, st, mm, s_st, s_mv)
                        if k == XN_:
                            dve.wait_ge(s_ps, a.of(7, 7))
                            normed(Fw[a.par], mm[:, 3, :], sscl).then_inc(s_xn, 1)
                        for c in range(2):
                            if k == S_[c]:
                                dve.wait_ge(s_s, a.of(2, c + 1))
                                dve.tensor_reduce(mx[:, c, :], B[c][:, :].rearrange("p (q s) -> p q s", q=QT), AX.X, ALU.max)\
                                   .then_inc(s_mx, 1)
                                dve.wait_ge(s_mx, a.of(2, c + 1))
                                dve.tensor_scalar(nb[:, c, :], mx[:, c, :], -SCALE, None, ALU.mult).then_inc(s_nb, 1)
                            if k == EXP_[c]:
                                dve.wait_ge(s_ex, a.of(2, c + 1))
                                dve.reciprocal(ri[:, c, :], rs[:, c, :]).then_inc(s_ri, 1)

            def normed(src, mean, scale):
                for r in range(TR):
                    c, odd = r // 2, r % 2
                    for lo, hi, at in (((0, P, 2 * P), (P, D, D)) if odd else ((0, D, 0),)):
                        last = dve.tensor_scalar(xn[:, c, at:at + hi - lo], src[:, r, lo:hi], mean[:, r:r + 1],
                                                 scale[:, r:r + 1], ALU.subtract, ALU.mult)
                return last

            def moments(g, stats, to, s_in, s_to):
                dve.wait_ge(s_in, g.of(1, 1))
                dve.tensor_tensor(to[:, 0, :], stats[:, :, 1], stats[:, :, 4], ALU.add)
                dve.tensor_tensor(to[:, 1, :], stats[:, :, 1], stats[:, :, 4], ALU.subtract)
                dve.tensor_tensor(to[:, 2, :], stats[:, :, 2], stats[:, :, 5], ALU.add).then_inc(s_to, 1)
                dve.wait_ge(s_to, g.of(3, 1))
                dve.tensor_scalar(to[:, 3, :], to[:, 0, :], 0.5, None, ALU.mult)
                dve.tensor_tensor(to[:, 4, :], to[:, 1, :], to[:, 1, :], ALU.mult).then_inc(s_to, 1)
                dve.wait_ge(s_to, g.of(3, 2))
                dve.scalar_tensor_tensor(to[:, 5, :], to[:, 4, :], D / 4.0, to[:, 2, :], ALU.mult, ALU.add).then_inc(s_to, 1)

            def route(b, part):
                c = (0, 6, 12)[part]

                def link(ins):
                    nonlocal c
                    c += 1
                    ins.then_inc(s_rc, 1)
                    dve.wait_ge(s_rc, b.of(NRC, c))

                def wide(i):
                    return rm[:, i, :].unsqueeze(2).to_broadcast([P, TR, NE])

                def largest(one, sel):
                    link(dve.tensor_reduce(rm[:, 2 * one, :], rt[:, sel, :, :], AX.X, ALU.max))
                    link(dve.tensor_tensor(rt[:, 4 + 4 * one, :, :], rt[:, sel, :, :], wide(2 * one), ALU.is_equal))

                if part == 0:
                    dve.wait_ge(s_re, b.of(1, 1))
                    link(dve.tensor_scalar(rt[:, 1, :, :], rt[:, 0, :, :], 1.0, None, ALU.add))
                    link(dve.reciprocal(rt[:, 2, :, :], rt[:, 1, :, :]))
                    link(dve.tensor_tensor(rt[:, 3, :, :], rt[:, 2, :, :],
                                           balb[:, :].unsqueeze(1).to_broadcast([P, TR, NE]), ALU.add))
                    largest(0, 3)
                    link(dve.tensor_tensor(rt[:, 5, :, :], rt[:, 4, :, :], rank[:, :, :], ALU.mult))
                    assert c == 6, c
                if part == 1:
                    link(dve.tensor_reduce(rm[:, 1, :], rt[:, 5, :, :], AX.X, ALU.max))
                    link(dve.tensor_tensor(rt[:, 6, :, :], rt[:, 5, :, :], wide(1), ALU.is_equal))
                    link(dve.scalar_tensor_tensor(rt[:, 7, :, :], rt[:, 6, :, :], -BIG, rt[:, 3, :, :], ALU.mult, ALU.add))
                    largest(1, 7)
                    link(dve.tensor_tensor(rt[:, 9, :, :], rt[:, 8, :, :], rank[:, :, :], ALU.mult))
                    assert c == 12, c
                if part == 2:
                    link(dve.tensor_reduce(rm[:, 3, :], rt[:, 9, :, :], AX.X, ALU.max))
                    link(dve.tensor_tensor(rt[:, 10, :, :], rt[:, 9, :, :], wide(3), ALU.is_equal))
                    link(dve.tensor_tensor(rt[:, 11:13, :, :], rt[:, 6:11:4, :, :],
                                           rt[:, 2, :, :].unsqueeze(1).to_broadcast([P, 2, TR, NE]), ALU.mult))
                    link(dve.tensor_reduce(rm[:, 4:6, :], rt[:, 11:13, :, :], AX.X, ALU.add))
                    link(dve.scalar_tensor_tensor(rm[:, 6, :], rm[:, 4, :], EPS_TOP, rm[:, 5, :], ALU.add, ALU.add))
                    link(dve.reciprocal(rm[:, 7, :], rm[:, 6, :]))
                    dve.tensor_tensor(rm[:, 8:10, :], rm[:, 4:6, :],
                                      rm[:, 7, :].unsqueeze(1).to_broadcast([P, 2, TR]), ALU.mult).then_inc(s_comb, 1)
                    assert c == NRC, c

            schedule(dve, step)

        @block.tensor
        def _(pe):
            pe.wait_ge(s_const, 12)
            pe.wait_ge(s_ones, 2)

            def split5(dst, s0h, s0l, s1, mvh, mvl, m1h, m1l, start, stop, tail=None):
                pe.matmul(dst, s0h, mvh, start=start, stop=False, skip_group_check=True)
                pe.matmul(dst, s0h, mvl, start=False, stop=False, skip_group_check=True)
                pe.matmul(dst, s0l, mvh, start=False, stop=False, skip_group_check=True)
                pe.matmul(dst, s1, m1h, start=False, stop=False, skip_group_check=True)
                last = pe.matmul(dst, s1, m1l, start=False, stop=stop and tail is None, skip_group_check=True)
                if tail is not None:
                    last = pe.matmul(dst, tail[0], tail[1], start=False, stop=stop, skip_group_check=True)
                return last

            def weights5(dst, w0h, w0l, w1h, w1l, xh, xl, x1):
                pe.matmul(dst, w0h, xh, start=True, stop=False)
                pe.matmul(dst, w0h, xl, start=False, stop=False)
                pe.matmul(dst, w0l, xh, start=False, stop=False)
                pe.matmul(dst, w1h, x1, start=False, stop=False)
                return pe.matmul(dst, w1l, x1, start=False, stop=True)

            def stage_a(a, k):
                later = not (isinstance(a.n, int) and a.n == 0)
                if k == GT_:
                    pe.wait_ge(s_gath[a.par], a.half * 64 + 64)
                    if later:
                        pe.wait_ge(s_vl, a.of(2, -1))
                    for c in range(2):
                        last = pe.transpose(A[0][:, c * P:(c + 1) * P],
                                            G[a.par][:, 2 * c:2 * c + 2, :].rearrange("p r k -> p (r k)"), ident[:, :])
                    last.then_inc(s_gt, 1)
                if k == E_:
                    if not later:
                        pe.wait_ge(s_wlo, N_PROJ)
                    else:
                        pe.wait_ge(s_vl, a.of(2, 0))
                    pe.wait_ge(s_gtl, a.of(1, 1))
                    for c in range(2):
                        for r in range(2):
                            dst = two(A[1 - c])[:, r, :]
                            lhs = GTs[:, (2 * c + r) * P:(2 * c + r + 1) * P]
                            pe.matmul(dst, lhs, PJh[:, :], start=True, stop=False)
                            last = pe.matmul(dst, lhs, PJl[:, :], start=False, stop=True)
                        last.then_inc(s_e, 1)
                if k == XT_:
                    pe.wait_ge(s_xn, a.of(1, 1))
                    for r in range(TR):
                        last = pe.transpose(A[1][:, r * P:(r + 1) * P], xn[:, r // 2, r % 2 * 2 * P:r % 2 * 2 * P + P], ident[:, :])
                    last.then_inc(s_xt, 1)
                    for c in range(2):
                        last = pe.transpose(A[0][:, c * P:(c + 1) * P], xn[:, c, P:2 * P], ident[:, :])
                    last.then_inc(s_xt, 1)
                if k in QK_:
                    c = QK_.index(k)
                    if c == 0:
                        if not later:
                            pe.wait_ge(s_wlo, N_QK)
                        pe.wait_ge(s_xl, a.of(2, 2))
                    if c == 2:
                        pe.wait_ge(s_qkl, a.of(3, 1))
                    cols = slice(c * P, (c + 1) * P)
                    weights5(A[(1 + c) % 2][:, :], QK0h[:, cols], QK0l[:, cols], QK1h[:, cols], QK1l[:, cols],
                             X0h[:, :], X0l[:, :], X1[:, :]).then_inc(s_qk, 1)
                if k in V_:
                    c = V_.index(k)
                    if c == 0 and not later:
                        pe.wait_ge(s_wlo, N_REST)
                    pe.wait_ge(s_qkl, a.of(3, 2 + c))
                    for r in range(2):
                        tok = slice((2 * c + r) * P, (2 * c + r + 1) * P)
                        last = split5(two(A[c])[:, r, :], X0h[:, tok], X0l[:, tok], X1[:, tok], WV0h[:, :], WV0l[:, :],
                                      WV1h[:, :], WV1l[:, :], True, True, tail=(ones[:, :], BVC[:, 0:D]))
                    last.then_inc(s_v, 1)
                if k in S_:
                    c = S_.index(k)
                    pe.wait_ge(s_qkl, a.of(3, 3))
                    if later:
                        pe.wait_ge(s_lg if c == 0 else s_cs, a.of(1, 0))
                    for q in range(QT):
                        qs = slice(c * SEQ + q * P, c * SEQ + (q + 1) * P)
                        ks = slice(c * SEQ, (c + 1) * SEQ)
                        last = split5(B[c][:, q * SEQ:(q + 1) * SEQ], Q0h[:, qs], Q0l[:, qs], Q1[:, qs], K0h[:, ks],
                                      K0l[:, ks], K1h[:, ks], K1l[:, ks], True, True)
                    last.then_inc(s_s, 1)

                if k in PT_:
                    c = PT_.index(k)
                    pe.wait_ge(s_ex, a.of(2, c + 1))
                    for q in range(QT):
                        for kt in range(QT):
                            last = pe.transpose(B[c][:, kt * SEQ + q * P:kt * SEQ + (q + 1) * P],
                                                Pr[:, c, q, kt * P:(kt + 1) * P], ident[:, :])
                    last.then_inc(s_pt, 1)

            WC_UNITS = [[(0, 0, 0), (1, 0, 2)], [(1, 0, 3), (0, 1, 1)], [(1, 1, 0), (0, 2, 2)], [(0, 2, 3), (1, 2, 1)]]

            def stage_b(b, k):
                if k in Y_:
                    c = Y_.index(k)
                    pe.wait_ge(s_ptl, b.of(2, c + 1))
                    pe.wait_ge(s_vl, b.of(2, 2))
                    for q in range(QT):
                        dst = two(B[c])[:, q, :]
                        for kt in range(QT):
                            qs, v = slice(q * P, (q + 1) * P), c * QT + kt
                            pe.matmul(dst, PTh[:, c, kt, qs], Vh[:, v, :], start=kt == 0, stop=False, skip_group_check=True)
                            pe.matmul(dst, PTh[:, c, kt, qs], Vl[:, v, :], start=False, stop=False, skip_group_check=True)
                            last = pe.matmul(dst, PTl[:, c, kt, qs], Vh[:, v, :], start=False, stop=kt == QT - 1,
                                             skip_group_check=True)
                    last.then_inc(s_y, 1)
                if k == WC_:
                    pe.wait_ge(s_yl, b.of(2, 2))
                    for c in range(2):
                        for r in range(2):
                            dst = two(B[c])[:, r, :]
                            for n, (qt, e3, w) in enumerate(WC_UNITS[2 * c + r]):
                                yh = Yh[:, qt, e3, :, :].rearrange("p s a -> p (s a)")
                                yl = Yl[:, qt, e3, :, :].rearrange("p s a -> p (s a)")
                                pe.matmul(dst, yh, WCh[:, w, :], start=n == 0, stop=False, skip_group_check=True)
                                pe.matmul(dst, yh, WCl[:, w, :], start=False, stop=False, skip_group_check=True)
                                pe.matmul(dst, yl, WCh[:, w, :], start=False, stop=False, skip_group_check=True)
                            last = pe.matmul(dst, ones[:, :], BVC[:, D:2 * D], start=False, stop=True, skip_group_check=True)
                        last.then_inc(s_wc, 1)
                if k == ZT_:
                    pe.wait_ge(s_xn2, b.of(1, 1))
                    for r in range(TR):
                        last = pe.transpose(B[0][:, r * P:(r + 1) * P], xn[:, r // 2, r % 2 * 2 * P:r % 2 * 2 * P + P], ident[:, :])
                    last.then_inc(s_zt, 1)
                    for c in range(2):
                        last = pe.transpose(B[1][:, c * P:(c + 1) * P], xn[:, c, P:2 * P], ident[:, :])
                    last.then_inc(s_zt, 1)
                if k == RT_:
                    pe.wait_ge(s_zl, b.of(2, 2))
                    z0h, z0l, z1 = Z0h[b.par], Z0l[b.par], Z1[b.par]
                    for r in range(TR):
                        tok = slice(r * P, (r + 1) * P)
                        dst = B[0][:, 2 * r * NE:2 * (r + 1) * NE]
                        w0, w1 = [w[:, :, :].rearrange("p a e -> p (a e)") for w in (RW0, RW1)]
                        pe.matmul(dst, z0h[:, tok], w0, start=True, stop=False, skip_group_check=True)
                        pe.matmul(dst, z0l[:, tok], w0, start=False, stop=False, skip_group_check=True)
                        last = pe.matmul(dst, z1[:, tok], w1, start=False, stop=True, skip_group_check=True)
                    last.then_inc(s_rt, 1)
                if k == CT_:
                    pe.wait_ge(s_root, b.of(3, 3))
                    pe.transpose(B[1][:, 0:P], rt[:, 10:14, :, :].rearrange("p i r e -> p (i r e)"), ident[:, :])\
                      .then_inc(s_ct, 1)

            def step(a, b, m, t):
                for k in range(NCH):
                    late_b = k in (ZT_, CT_)
                    if b is not None and not late_b:
                        stage_b(b, k)
                    if a is not None:
                        stage_a(a, k)
                    if m is not None:
                        if k == 0:
                            pe.wait_ge(s_zl, m.of(2, 2))
                            if t is None:
                                pe.wait_ge(s_wlo, N_ALL)
                        if t is not None or k >= 2:
                            pe.wait_ge(s_r, m.of(NCH, k - 1))
                        cols = slice(k * P, (k + 1) * P)
                        weights5(UB[k % 2][:, :], UP0h[:, cols], UP0l[:, cols], UP1h[:, cols], UP1l[:, cols],
                                 Z0h[m.par][:, :], Z0l[m.par][:, :], Z1[m.par][:, :]).then_inc(s_up, 1)
                    if b is not None and late_b:
                        stage_b(b, k)
                    for j, g in downs_at(k, m, t):
                        pe.wait_ge(s_ul, g.of(NCH, j + 1))
                        if j == 0 and t is not None:
                            pe.wait_ge(s_ot, g.of(2, 0))
                        for c in range(TR):
                            dst = two(AC[c // 2])[:, c % 2, :]
                            tok = slice(c * P, (c + 1) * P)
                            for n, (u, w) in enumerate(((Uh, DNh), (Uh, DNl), (Ul, DNh))):
                                last = pe.matmul(dst, u[j % NU][:, tok], w[:, j, :], start=j == 0 and n == 0 and c % 2 == 0,
                                                 stop=j == NCH - 1 and n == 2, skip_group_check=True)
                        last.then_inc(s_dn, 1)

            schedule(pe, step)


_IN = ["x", "coords", "w_proj", "norm_w", "w_qk", "b_qk", "w_v", "b_v", "w_c", "b_c", "w_up", "w_down", "w_router", "b_bal"]


def kernel(**inputs):
    import numpy as np
    import concourse.bacc as bacc
    from concourse.bass_utils import run_bass_kernel_spmd

    a = {k.replace("L0_", ""): np.asarray(v) for k, v in inputs.items()}
    wq, wk = a["attn_Wq"].T, a["attn_Wk"].T
    bq, bk = a["attn_bq"], a["attn_bk"]
    up = np.concatenate([a["ffn_w1"].transpose(1, 0, 2).reshape(D, NE * D), a["ffn_w_fc_sh"]], axis=1)
    down = np.concatenate([a["ffn_w2"].reshape(NE * D, D), a["ffn_w_proj_sh"]], axis=0)
    laid = {
        "x": a["x"], "coords": a["tok_basin_coords"], "w_proj": a["tok_proj_w"].T, "norm_w": a["tok_norm_w"],
        "w_qk": np.concatenate([wq[:, :P], wk[:, :P], wq[:, P:], wk[:, P:]], axis=1),
        "b_qk": np.concatenate([bq[:P], bk[:P], bq[P:], bk[P:]]).reshape(3, P).T,
        "w_v": a["attn_Wv"].T, "b_v": a["attn_bv"], "w_c": a["attn_Wc"].T, "b_c": a["attn_bc"],
        "w_up": np.pad(up, ((0, 0), (0, HP - HID))), "w_down": np.pad(down, ((0, HP - HID), (0, 0))),
        "w_router": a["ffn_router_w"].T, "b_bal": a["ffn_balance_bias"],
    }
    nc = bacc.Bacc("TRN2", target_bir_lowering=False, num_devices=1)
    arrays, args = {}, []
    for name in _IN:
        v = np.ascontiguousarray(laid[name])
        arrays[f"in_{name}"] = v
        args.append(nc.dram_tensor(f"in_{name}", v.shape, mybir.dt.from_np(v.dtype), kind="ExternalInput").ap())
    args.append(nc.dram_tensor("out_y", (BATCH, SEQ, D), mybir.dt.float32, kind="ExternalOutput").ap())
    tower_kernel(nc, *args)
    r = run_bass_kernel_spmd(nc, [arrays], core_ids=[0])
    return r.results[0]["out_y"]
```

```python
import concourse.bass as bass
from concourse import mybir
from contextlib import ExitStack

P = 128
D = 192
KD = 64
DR = D - P
VOCAB = 32000
BATCH, SEQ = 16, 256
GT = 512
STEPS = BATCH * SEQ // GT
TR = GT // P
SG = GT // SEQ
QT = SEQ // P
NE = 8
HID = (NE + 1) * D
NCH = -(-HID // P)
ECH = NE * D // P
HP = NCH * P
LAG = 3
NU = 3
SCALE = float(D) ** -0.5
EPS_RMS, EPS_LN, EPS_TOP = 1e-8, 1e-5, 1e-20
BIG = 3.0e38


class Group:

    def __init__(self, i, off):
        self.n = 2 * i + off if off else 2 * i
        self.par = off % 2
        self.half = i + off // 2 if off // 2 else i

    def of(self, each, k):
        return self.n * each + k if k else self.n * each


def tower_kernel(nc, x, coords, w_proj, norm_w, w_qk, b_qk, w_v, b_v, w_c, b_c, w_up, w_down, w_router, b_bal, out):
    f32, f32r, i32 = mybir.dt.float32, mybir.dt.float32r, mybir.dt.int32
    ALU, ACT, AX = mybir.AluOpType, mybir.ActivationFunctionType, mybir.AxisListType

    ids_v = x.rearrange("b s -> (b s)").rearrange("(n p r) -> p n r", p=P, r=TR)
    out_v = out.rearrange("b s d -> (b s d)").rearrange("(n p f) -> n p f", p=P, f=TR * D)
    comb_dram = nc.dram_tensor("comb_scratch", (2, TR, NE, P), f32).ap()

    ctx = ExitStack()
    with ctx:
        def sb(name, shape, dt=f32):
            return ctx.enter_context(nc.sbuf_tensor(name, shape, dt))

        def sem(name):
            return ctx.enter_context(nc.semaphore(name))

        ident = sb("ident", [P, P])
        fold = sb("fold", [P, DR])
        ones = sb("ones", [P, P], f32r)
        nhalf = sb("nhalf", [P, TR])
        phalf = sb("phalf", [P, 1])
        rank = sb("rank", [P, TR, NE])
        normw = sb("normw", [P, D])
        balb = sb("balb", [P, NE])
        bqk = sb("bqk", [P, 3])
        PJh, PJl = sb("PJh", [P, D], f32r), sb("PJl", [P, D], f32r)
        QK0h, QK0l, QK1h, QK1l = [sb(f"QK{s}", [P, 2 * D], f32r) for s in ("0h", "0l", "1h", "1l")]
        WV0h, WV0l, WV1h, WV1l = [sb(f"WV{s}", [P, D], f32r) for s in ("0h", "0l", "1h", "1l")]
        WCh, WCl = [sb(f"WC{s}", [P, 4, D], f32r) for s in ("h", "l")]
        RW0, RW1 = [sb(f"RW{s}", [P, 2, NE], f32r) for s in ("0", "1")]
        BVC = sb("BVC", [P, 2 * D], f32r)
        UP0h, UP0l, UP1h, UP1l = [sb(f"UP{s}", [P, HP], f32r) for s in ("0h", "0l", "1h", "1l")]
        DN0h, DN0l, DN1 = [sb(f"DN{s}", [P, NCH, P], f32r) for s in ("0h", "0l", "1")]
        ids = sb("ids", [P, STEPS, TR], i32)
        rows = sb("rows", [P, STEPS, TR], i32)
        row_now = [sb(f"row_now{i}", [P, TR], i32) for i in range(2)]
        G = [sb(f"G{i}", [P, TR, KD]) for i in range(2)]
        ss = sb("ss", [P, TR])
        Fw = [sb(f"Fw{i}", [P, TR, D]) for i in range(2)]
        st = sb("st", [P, TR, 6])
        idf, neg = [Fw[0][:, i, 0:STEPS * TR].rearrange("p (n r) -> p n r", r=TR) for i in range(2)]
        mm = sb("mm", [P, 6, TR])
        sA = sb("sA", [P, 4, TR])
        sr1 = [sb(f"sr1{i}", [P, TR]) for i in range(2)]
        sscl = sb("sscl", [P, TR])
        sbias = sb("sbias", [P, TR])
        X0h, X0l, X1 = [sb(f"X{s}", [P, GT], f32r) for s in ("0h", "0l", "1")]
        QB, KB = sb("QB", [P, 2, GT], f32r), sb("KB", [P, 2, GT], f32r)
        Q0h, Q0l, K0h, K0l = QB[:, 0, :], QB[:, 1, :], KB[:, 0, :], KB[:, 1, :]
        Q1 = sb("Q1", [P, GT], f32r)
        GTs = Q1
        K1h, K1l = sb("K1h", [P, GT], f32r), sb("K1l", [P, GT], f32r)
        Vh, Vl = [sb(f"V{s}", [P, TR, D], f32r) for s in ("h", "l")]
        mx = sb("mx", [P, SG, QT])
        nb = sb("nb", [P, SG, QT])
        rs = sb("rs", [P, SG, QT])
        ri = sb("ri", [P, SG, QT])
        Pr = sb("Pr", [P, SG, QT, SEQ])
        xn = Pr[:, :, :, :].rearrange("p a b c -> p (a b c)")[:, 0:TR * D].rearrange("p (c w) -> p c w", c=2)
        Yh, Yl = [t[:, :, :].rearrange("p a b -> p (a b)")[:, 0:TR * D]
                  .rearrange("p (q c s a) -> p q c s a", q=QT, c=3, s=SG) for t in (QB, KB)]
        PTh, PTl = [sb(f"PT{s}", [P, SG, QT, SEQ], f32r) for s in ("h", "l")]
        h2 = [sb(f"h2{i}", [P, TR, D]) for i in range(2)]
        st2 = sb("st2", [P, TR, 6])
        mm2 = sb("mm2", [P, 6, TR])
        ve2 = sb("ve2", [P, TR])
        s2 = sb("s2", [P, TR])
        s2bias = sb("s2bias", [P, TR])
        Z0h, Z0l, Z1 = [[sb(f"Z{s}_{i}", [P, GT], f32r) for i in range(2)] for s in ("0h", "0l", "1")]
        rt = sb("rt", [P, 14, TR, NE])
        rm = sb("rm", [P, 12, TR])
        combT = sb("combT", [P, P])
        combB = [sb(f"combB{i}", [P, ECH, GT]) for i in range(2)]
        OUT = [t[:, :, :].rearrange("p a b -> p (a b)")[:, 0:TR * D] for t in combB]
        ACS = [[t[:, 2 + i, :] for i in range(2)] for t in combB]
        R = [sb(f"R{i}", [P, GT]) for i in range(2)]
        U = [sb(f"U{i}", [P, GT]) for i in range(2)]
        Uh, Ul = [[sb(f"U{s}{i}", [P, GT], f32r) for i in range(NU)] for s in ("h", "l")]
        raw0 = combB[0][:, :, :].rearrange("p a b -> p (a b)")
        raw1 = combB[1][:, :, :].rearrange("p a b -> p (a b)")
        at = [0]

        def raw(base, n):
            at[0] += n
            assert at[0] <= ECH * GT
            return base[:, at[0] - n:at[0]]
        rPJ = raw(raw0, D)
        rQK0, rQK1 = raw(raw0, 2 * D), raw(raw0, 2 * D)
        rWV0, rWV1 = raw(raw0, D), raw(raw0, D)
        rWC = raw(raw0, 4 * D)
        rRW0, rRW1 = raw(raw0, NE), raw(raw0, NE)
        rB = raw(raw0, 2 * D)
        rDN = raw(raw0, NCH * D)
        at[0] = 0
        rUP0, rUP1 = raw(raw1, HP), raw(raw1, HP)

        def bank(name):
            return ctx.enter_context(nc.psum_tensor(name, [P, 512], f32))
        A = [bank("A0"), bank("A1")]
        B = [bank("B0"), bank("B1")]
        UB = [bank("U0p"), bank("U1p")]
        AC = [bank("acc0"), bank("acc1")]

        def two(t):
            return t[:, 0:2 * D].rearrange("p (a d) -> p a d", a=2)

        def halves(t):
            return t[:, 0:2 * P].rearrange("q (c p) -> q c p", c=2)

        def pair(t):
            return t[:, :].rearrange("q (c o p) -> q o c p", c=2, o=2)

        def pair_tok(t):
            return t[:, :].rearrange("q (p c o) -> q o c p", c=2, o=2)

        s_raw = [sem(f"raw_loaded{i}") for i in range(4)]
        s_zero = sem("stage_zeroed")
        s_const = sem("constants_made")
        s_ones = sem("ones_made")
        s_ids = sem("ids_loaded")
        s_rows = sem("rows_clamped")
        s_whi = sem("weight_hi_made")
        s_wlo = sem("weight_lo_made")
        s_gath = [sem(f"gathered{i}") for i in range(2)]
        s_rowc = sem("row_numbers_copied")
        s_gt = sem("pe_basin_transposed")
        s_gth = sem("basin_hi_made")
        s_gtl = sem("basin_lo_made")
        s_e = sem("pe_embedded")
        s_sq = sem("squares_summed")
        s_fw = sem("embedding_weighted")
        s_st = sem("stats_made")
        s_mv = sem("moments_made")
        s_ps = sem("pool_scale_steps")
        s_xn = sem("normed")
        s_xna = sem("normed_by_act")
        s_xt = sem("pe_normed_transposed")
        s_xh = sem("normed_hi_made")
        s_xl = sem("normed_lo_made")
        s_qk = sem("pe_qk_made")
        s_qkh = sem("qk_hi_made")
        s_qkl = sem("qk_lo_made")
        s_v = sem("pe_v_made")
        s_vh = sem("v_hi_made")
        s_vl = sem("v_lo_made")
        s_s = sem("pe_scores_made")
        s_mx = sem("row_max_found")
        s_nb = sem("exp_bias_made")
        s_ex = sem("exps_made")
        s_ri = sem("row_sums_inverted")
        s_pt = sem("pe_probabilities_transposed")
        s_pth = sem("probability_hi_made")
        s_ptl = sem("probability_lo_made")
        s_y = sem("pe_attended")
        s_yh = sem("attended_hi_made")
        s_yl = sem("attended_lo_made")
        s_wc = sem("pe_attention_out_made")
        s_h2 = sem("second_residual_made")
        s_st2 = sem("second_stats_made")
        s_mv2 = sem("second_moments_made")
        s_p2 = sem("pool_second_scale_steps")
        s_xn2 = sem("second_normed")
        s_xn2a = sem("second_normed_by_act")
        s_zt = sem("pe_second_normed_transposed")
        s_zh = sem("second_normed_hi_made")
        s_zl = sem("second_normed_lo_made")
        s_rt = sem("pe_logits_made")
        s_lg = sem("logit_halves_added")
        s_re = sem("logit_exps_made")
        s_rc = sem("router_steps")
        s_comb = sem("shares_made")
        s_root = sem("root_steps")
        s_ct = sem("pe_combine_transposed")
        s_cs = sem("combine_copied")
        s_cd = sem("combine_stored")
        s_cb = [[sem(f"combine_spread{i}_{g}") for g in range(NE // 2)] for i in range(2)]
        s_up = sem("pe_up_made")
        s_r = sem("relu_made")
        s_t = sem("hidden_weighted")
        s_u = sem("hidden_squared")
        s_uh = sem("hidden_hi_made")
        s_ul = sem("hidden_lo_made")
        s_dn = sem("pe_down_made")
        s_acc = sem("accumulators_copied")
        s_res = sem("residual_copied")
        s_op = sem("pe_output_transposed")
        s_ot = sem("output_made")
        s_out = sem("output_stored")
        NRC = 18

        TICKS = 10
        AT = {
            "pe": {"UP": 0, "DOWN": 7, "GT": 2, "E": 16, "XT": 51, "QK": (60, 70, 79), "V": (87, 122),
                   "S": (92, 102), "PT": (114, 123), "Y": (1, 11), "WC": 23, "ZT": 40, "RT": 51, "CT": 95, "OUT": 30},
            "act": {"SQUARE": 5, "RELU": 3, "HI": 8, "GT": 3, "E": 15, "XT": 48, "QK": (67, 77, 80), "V": (89, 121),
                    "EXP": (98, 113), "PT": (108, 119), "Y": (2, 11), "ZT": 39, "RT": 53, "CT": 92, "XN2": 35,
                    "XN": 48, "ACC": 19},
            "dve": {"LO": 9, "OUT": 29, "GT": 1, "E": 16, "XT": 51, "QK": (61, 71, 81), "V": (93, 121),
                    "PT": (104, 119), "BN": 38, "XN": 48, "S": (86, 107), "EXP": (108, 110), "Y": (0, 13), "WC": 22,
                    "RT": 52, "ZT": 45, "XN2": 31, "ROUTE": (52, 68, 77)},
            "pool": {"WEIGH": 6, "RMS": 34, "LN": 43, "LN2": 29, "ROOT": 85, "GATHER": (50, 66, 92, 126), "RES": 11},
        }
        START = {
            "pe": {"UP": 7, "DOWN": 3, "GT": 2, "E": 12, "XT": 62, "QK": (62, 77, 78), "V": (92, 119),
                   "S": (92, 102), "PT": (112, 123), "Y": (5, 16), "WC": 16, "ZT": 51, "RT": 51, "CT": 100},
            "act": {"SQUARE": 8, "RELU": 7, "HI": 1, "GT": 1, "E": 14, "XT": 60, "QK": (70, 71, 80), "V": (92, 121),
                    "EXP": (99, 114), "PT": (111, 122), "Y": (7, 17), "ZT": 47, "RT": 52, "CT": 92, "XN2": 31,
                    "XN": 48},
            "dve": {"LO": 5, "GT": 1, "E": 9, "XT": 60, "QK": (66, 72, 81), "V": (96, 121), "PT": (111, 133),
                    "BN": 22, "XN": 49, "S": (98, 106), "EXP": (108, 113), "Y": (2, 17), "WC": 23, "RT": 52,
                    "ZT": 47, "XN2": 24, "ROUTE": (52, 71, 79)},
            "pool": {"WEIGH": 7, "RMS": 29, "LN": 46, "LN2": 29, "ROOT": 85, "GATHER": (53, 78, 99, 115)},
        }
        FIRST = {
            "pe": {"UP": 7, "DOWN": 7, "GT": 7, "E": 7, "XT": 52, "QK": (62, 72, 81), "V": (92, 122), "S": (92, 102),
                   "PT": (112, 123)},
            "act": {"SQUARE": 8, "RELU": 7, "HI": 8, "GT": 6, "E": 9, "XT": 50, "QK": (70, 71, 80), "V": (92, 121),
                    "EXP": (101, 115), "PT": (111, 122), "XN": 30},
            "dve": {"LO": 9, "GT": 6, "E": 11, "XT": 50, "QK": (61, 71, 81), "V": (96, 121), "PT": (111, 135),
                    "BN": 33, "XN": 36, "S": (98, 106), "EXP": (108, 127)},
            "pool": {"WEIGH": 6, "RMS": 14, "LN": 46, "GATHER": (53, 78, 97, 115)},
        }
        END = {
            "pe": {"UP": 0, "DOWN": 3, "Y": (1, 11), "WC": 23, "ZT": 40, "RT": 51, "CT": 105, "OUT": 31},
            "act": {"SQUARE": 5, "RELU": 3, "HI": 8, "Y": (2, 11), "ZT": 39, "RT": 53, "CT": 102, "XN2": 35,
                    "ACC": 18},
            "dve": {"LO": 9, "OUT": 29, "Y": (3, 13), "WC": 22, "RT": 52, "ZT": 45, "XN2": 31, "ROUTE": (52, 68, 77)},
            "pool": {"WEIGH": 5, "LN2": 26, "ROOT": 95, "RES": 8},
        }

        def table(a, b, m):
            if a is None:
                return END
            if m is not None:
                return AT
            return FIRST if b is None else START

        block = ctx.enter_context(nc.Block())

        def schedule(eng, step):
            step(Group(0, 0), None, None, None)
            step(Group(0, 1), Group(0, 0), None, None)
            step(Group(0, 2), Group(0, 1), Group(0, 0), None)
            step(Group(0, 3), Group(0, 2), Group(0, 1), Group(0, 0))
            with eng.Fori(1, STEPS // 2 - 1) as i:
                step(Group(i, 2), Group(i, 1), Group(i, 0), Group(i, -1))
                step(Group(i, 3), Group(i, 2), Group(i, 1), Group(i, 0))
            last = STEPS // 2 - 1
            step(None, Group(last, 1), Group(last, 0), Group(last, -1))
            step(None, None, Group(last, 1), Group(last, 0))
            step(None, None, None, Group(last, 1))

        def chunk_at(k, lag, m, t):
            return (k - lag, m) if k >= lag else (k - lag + NCH, t)

        XN_PARTS = [[(2 * c, 0, D, 0), (2 * c + 1, 0, P, 2 * P), (2 * c + 1, P, D, D)] for c in range(2)]

        def downs_at(k, m, t):
            late = {0: (ECH - 1, ECH), 1: (ECH + 1,)}
            at = [(k - LAG, m)] if k >= LAG else [(j, t) for j in late.get(k, ())]
            return [(j, g) for j, g in at if g is not None]

        @block.sync
        def _(sp):
            sp.dma_start(ids[:, :, :], ids_v).then_inc(s_ids, 16)
            for half in (0, KD):
                sp.dma_start(rPJ[half:half + KD, :], w_proj).then_inc(s_raw[0], 16)
            sp.dma_start(normw[:, :], norm_w.partition_broadcast(P)).then_inc(s_raw[0], 16)
            sp.dma_start(rQK0, w_qk[0:P, :]).then_inc(s_raw[1], 16)
            for half in (0, KD):
                sp.dma_start(rQK1[half:half + DR, :], w_qk[P:D, :]).then_inc(s_raw[1], 16)
            sp.dma_start(bqk[:, :], b_qk).then_inc(s_raw[1], 16)
            sp.dma_start(rWV0, w_v[0:P, :]).then_inc(s_raw[2], 16)
            sp.dma_start(rRW0, w_router[0:P, :]).then_inc(s_raw[2], 16)
            for half in (0, KD):
                sp.dma_start(rWV1[half:half + DR, :], w_v[P:D, :]).then_inc(s_raw[2], 16)
                sp.dma_start(rRW1[half:half + DR, :], w_router[P:D, :]).then_inc(s_raw[2], 16)
            sp.dma_start(balb[:, :], b_bal.partition_broadcast(P)).then_inc(s_raw[2], 16)
            sp.wait_ge(s_zero, 2)
            sp.dma_start(rWC[:, 0:D], w_c[0:P, :]).then_inc(s_raw[2], 16)
            sp.dma_start(rWC[:, D:2 * D], w_c[KD:KD + P, :]).then_inc(s_raw[2], 16)
            sp.dma_start(rWC[0:KD, 2 * D:3 * D], w_c[P:D, :]).then_inc(s_raw[2], 16)
            sp.dma_start(rWC[KD:P, 3 * D:4 * D], w_c[0:KD, :]).then_inc(s_raw[2], 16)
            for row in (0, 32):
                sp.dma_start(rB[row:row + 1, 0:D], b_v.rearrange("(a n) -> a n", a=1)).then_inc(s_raw[2], 16)
                sp.dma_start(rB[row:row + 1, D:2 * D], b_c.rearrange("(a n) -> a n", a=1)).then_inc(s_raw[2], 16)
            sp.dma_start(rUP0, w_up[0:P, :]).then_inc(s_raw[3], 16)
            for half in (0, KD):
                sp.dma_start(rUP1[half:half + DR, :], w_up[P:D, :]).then_inc(s_raw[3], 16)
            sp.dma_start(rDN.rearrange("p (c n) -> p c n", c=NCH),
                         w_down.rearrange("(c p) n -> p c n", p=P)).then_inc(s_raw[3], 16)

            def step(a, b, m, t):
                if t is not None:
                    sp.wait_ge(s_ot, t.of(2, 2))
                    sp.dma_start(out_v[t.n, :, :], OUT[t.par]).then_inc(s_out, 16)
                if b is not None:
                    sp.wait_ge(s_cs, b.of(1, 1))
                    sp.dma_start(comb_dram[b.par].rearrange("r e p -> (r e) p"), combT[P - TR * NE:P, :]).then_inc(s_cd, 16)
                    sp.wait_ge(s_cd, b.of(16, 16))
                    if t is not None:
                        sp.wait_ge(s_out, t.of(16, 16))
                    for g in range(NE // 2):
                        for lo, hi, j, odd in ((0, P, 0, 0), (0, KD, 1, 0), (KD, P, 1, 1), (0, P, 2, 1)):
                            sp.dma_start(combB[b.par][lo:hi, 3 * g + j, :].rearrange("q (r p) -> q r p", r=TR),
                                         comb_dram[b.par, :, 2 * g + odd, :].partition_broadcast(hi - lo))\
                              .then_inc(s_cb[b.par][g], 16)

            schedule(sp, step)
            sp.wait_ge(s_out, 16 * STEPS)

        @block.gpsimd
        def _(pool):
            pool.memset(rWC, 0.0).then_inc(s_zero, 1)
            pool.memset(rB, 0.0).then_inc(s_zero, 1)
            pool.memset(ident[:, :], 0.0).then_inc(s_const, 1)
            pool.wait_ge(s_const, 1)
            pool.affine_select(out=ident[:, :], in_=ident[:, :], compare_op=ALU.not_equal, fill=1.0, base=0,
                               pattern=[[-1, P]], channel_multiplier=1).then_inc(s_const, 1)
            pool.memset(fold[:, :], 0.0).then_inc(s_const, 1)
            for n, base in enumerate((0, -DR)):
                pool.wait_ge(s_const, 3 + n)
                pool.affine_select(out=fold[:, :], in_=fold[:, :], compare_op=ALU.not_equal, fill=1.0, base=base,
                                   pattern=[[-1, DR]], channel_multiplier=1).then_inc(s_const, 1)
            pool.memset(nhalf[:, :], -0.5).then_inc(s_const, 1)
            pool.memset(phalf[:, :], 0.5).then_inc(s_const, 1)
            for e in range(NE):
                pool.memset(rank[:, :, e:e + 1], float(NE - e)).then_inc(s_const, 1)

            def gather(g, r):
                if r == 0:
                    pool.tensor_copy(row_now[g.par][:, :], rows[:, g.n, :]).then_inc(s_rowc, 1)
                    pool.wait_ge(s_rowc, g.of(1, 1))
                    if not (isinstance(g.n, int) and g.n < 2):
                        pool.wait_ge(s_gt, g.of(1, -1))
                pool.indirect_dma_start(out=G[g.par][:, r, :], out_offset=None, in_=coords,
                                        in_offset=bass.IndirectOffsetOnAxis(ap=row_now[g.par][:, r:r + 1], axis=0))\
                    .then_inc(s_gath[g.par], 16)

            pool.wait_ge(s_const, 15)
            pool.wait_ge(s_rows, 5)
            for r in range(TR):
                gather(Group(0, 0), r)

            def step(a, b, m, t, following):
                W = table(a, b, m)["pool"]
                for now in range(NCH * TICKS):
                    k = now // TICKS
                    if a is not None and now == W["RMS"]:
                        pool.wait_ge(s_sq, a.of(2, 2))
                        pool.tensor_scalar(sA[:, 0, :], ss[:, :], 1.0 / D, EPS_RMS, ALU.mult, ALU.add).then_inc(s_ps, 1)
                        pool.wait_ge(s_ps, a.of(8, 1))
                        pool.tensor_tensor(sr1[a.par][:, :], sA[:, 0, :], nhalf[:, :], ALU.pow).then_inc(s_ps, 1)
                        pool.wait_ge(s_ps, a.of(8, 2))
                        pool.tensor_tensor(sA[:, 1, :], sr1[a.par][:, :], sr1[a.par][:, :], ALU.mult).then_inc(s_ps, 1)
                        pool.wait_ge(s_ps, a.of(8, 3))
                    if a is not None and now == W["LN"]:
                        pool.wait_ge(s_mv, a.of(3, 3))
                        pool.tensor_tensor(sA[:, 2, :], sA[:, 1, :], mm[:, 5, :], ALU.mult).then_inc(s_ps, 1)
                        pool.wait_ge(s_ps, a.of(8, 4))
                        pool.tensor_scalar(sA[:, 3, :], sA[:, 2, :], 1.0 / D, EPS_LN, ALU.mult, ALU.add).then_inc(s_ps, 1)
                        pool.wait_ge(s_ps, a.of(8, 5))
                        pool.tensor_tensor(sA[:, 0, :], sA[:, 3, :], nhalf[:, :], ALU.pow).then_inc(s_ps, 1)
                        pool.wait_ge(s_ps, a.of(8, 6))
                        pool.tensor_tensor(sscl[:, :], sA[:, 0, :], sr1[a.par][:, :], ALU.mult).then_inc(s_ps, 1)
                        pool.wait_ge(s_ps, a.of(8, 7))
                        pool.tensor_tensor(sbias[:, :], sscl[:, :], mm[:, 3, :], ALU.mult).then_inc(s_ps, 1)
                    if b is not None and now == W["LN2"]:
                        pool.wait_ge(s_mv2, b.of(3, 3))
                        pool.tensor_scalar(ve2[:, :], mm2[:, 5, :], 1.0 / D, EPS_LN, ALU.mult, ALU.add).then_inc(s_p2, 1)
                        pool.wait_ge(s_p2, b.of(3, 1))
                        pool.tensor_tensor(s2[:, :], ve2[:, :], nhalf[:, :], ALU.pow).then_inc(s_p2, 1)
                        pool.wait_ge(s_p2, b.of(3, 2))
                        pool.tensor_tensor(s2bias[:, :], s2[:, :], mm2[:, 3, :], ALU.mult).then_inc(s_p2, 1)
                    if b is not None and now == W["ROOT"]:
                        pool.wait_ge(s_comb, b.of(1, 1))
                        pool.tensor_tensor(rm[:, 10:12, :], rm[:, 8:10, :],
                                           phalf[:, 0:1].unsqueeze(2).to_broadcast([P, 2, TR]), ALU.pow).then_inc(s_root, 1)
                        pool.wait_ge(s_root, b.of(3, 1))
                        pool.tensor_tensor(rt[:, 11:13, :, :], rt[:, 6:11:4, :, :],
                                           rm[:, 10:12, :].unsqueeze(3).to_broadcast([P, 2, TR, NE]), ALU.mult).then_inc(s_root, 1)
                        pool.wait_ge(s_root, b.of(3, 2))
                        pool.tensor_tensor(rt[:, 13, :, :], rt[:, 11, :, :], rt[:, 12, :, :], ALU.add).then_inc(s_root, 1)
                    if m is not None and k < ECH and now % TICKS == W["WEIGH"]:
                        if k % 3 == 0:
                            pool.wait_ge(s_cb[m.par][k // 3], m.half * 64 + 64)
                        pool.wait_ge(s_r, m.of(NCH, k + 1))
                        if t is not None or k >= 2:
                            pool.wait_ge(s_ul, m.of(NCH, k - 1))
                        pool.tensor_tensor(U[k % 2][:, :], R[k % 2][:, :], combB[m.par][:, k, :], ALU.mult)\
                            .then_inc(s_t, 1)
                    if t is not None and now == W["RES"]:
                        pool.wait_ge(s_h2, t.of(2, 2))
                        pool.tensor_copy(OUT[t.par], h2[t.par][:, :, :].rearrange("p r d -> p (r d)")).then_inc(s_res, 1)
                    if following is not None and now in W["GATHER"]:
                        gather(following, W["GATHER"].index(now))

            step(Group(0, 0), None, None, None, Group(0, 1))
            step(Group(0, 1), Group(0, 0), None, None, Group(0, 2))
            step(Group(0, 2), Group(0, 1), Group(0, 0), None, Group(0, 3))
            step(Group(0, 3), Group(0, 2), Group(0, 1), Group(0, 0), Group(0, 4))
            with pool.Fori(1, STEPS // 2 - 2) as i:
                step(Group(i, 2), Group(i, 1), Group(i, 0), Group(i, -1), Group(i, 3))
                step(Group(i, 3), Group(i, 2), Group(i, 1), Group(i, 0), Group(i, 4))
            i = STEPS // 2 - 2
            step(Group(i, 2), Group(i, 1), Group(i, 0), Group(i, -1), Group(i, 3))
            step(Group(i, 3), Group(i, 2), Group(i, 1), Group(i, 0), None)
            last = STEPS // 2 - 1
            step(None, Group(last, 1), Group(last, 0), Group(last, -1), None)
            step(None, None, Group(last, 1), Group(last, 0), None)
            step(None, None, None, Group(last, 1), None)

        def pieces(rawt, hi, lo, n, w=GT):
            return [(rawt[:, c:min(c + w, n)], hi[:, c:min(c + w, n)], lo[:, c:min(c + w, n)]) for c in range(0, n, w)]

        flatC = [t[:, :, :].rearrange("p a b -> p (a b)") for t in (WCh, WCl)]
        rDNc = rDN.rearrange("p (c n) -> p c n", c=NCH)
        down_w = ([(rDNc[:, c:min(c + 4, NCH), 0:P], DN0h[:, c:min(c + 4, NCH), :], DN0l[:, c:min(c + 4, NCH), :])
                   for c in range(0, NCH, 4)] +
                  [(rDNc[:, c:c + 7, P:D], DN1[:, c:c + 7, 0:DR], DN1[:, c:c + 7, DR:P]) for c in range(0, NCH, 7)])
        proj_w = pieces(rPJ, PJh, PJl, D)
        qk_w = pieces(rQK0, QK0h, QK0l, 2 * D) + pieces(rQK1, QK1h, QK1l, 2 * D)
        rest_w = (pieces(rWV0, WV0h, WV0l, D) + pieces(rWV1, WV1h, WV1l, D) +
                  pieces(rWC, flatC[0], flatC[1], 4 * D, 4 * D) +
                  [(r, w[:, 0, :], w[:, 1, :]) for r, w in ((rRW0, RW0), (rRW1, RW1))])
        mlp_w = pieces(rUP0, UP0h, UP0l, HP) + pieces(rUP1, UP1h, UP1l, HP) + down_w
        QK_LOADS, REST_LOADS, MLP_LOADS = 4, 15, 4
        QK_SLOT, REST_SLOT, MLP_SLOT = 3, 6, 6
        MLP_END = 14
        N_PROJ = len(proj_w)
        N_QK = N_PROJ + len(qk_w)
        N_REST = N_QK + len(rest_w) + 1
        N_ALL = N_REST + len(mlp_w)

        def mlp_split_at(k):
            if not MLP_SLOT <= k < MLP_END:
                return []
            lo, hi = [x * len(mlp_w) // (MLP_END - MLP_SLOT) for x in (k - MLP_SLOT, k - MLP_SLOT + 1)]
            return [(N_REST + x, mlp_w[x]) for x in range(lo, hi)]

        @block.scalar
        def _(act):
            act.preload_act_table(ACT.Exp)
            act.wait_ge(s_raw[0], 48)
            for src, hi, lo in proj_w:
                act.activation(hi, src, ACT.Copy).then_inc(s_whi, 1)

            def split(k):
                if k == QK_SLOT:
                    act.wait_ge(s_raw[1], 16 * QK_LOADS)
                    for src, hi, lo in qk_w:
                        act.activation(hi, src, ACT.Copy).then_inc(s_whi, 1)
                if k == REST_SLOT:
                    act.wait_ge(s_raw[2], 16 * REST_LOADS)
                    for src, hi, lo in rest_w:
                        act.activation(hi, src, ACT.Copy).then_inc(s_whi, 1)
                    act.activation(BVC[:, :], rB, ACT.Copy).then_inc(s_whi, 1)
                if k == MLP_SLOT:
                    act.wait_ge(s_raw[3], 16 * MLP_LOADS)
                for n, (src, hi, lo) in mlp_split_at(k):
                    act.activation(hi, src, ACT.Copy).then_inc(s_whi, 1)

            def normed(src, bias, scale):
                for r, lo, hi, at in XN_PARTS[1]:
                    last = act.activation(xn[:, 1, at:at + hi - lo], src[:, r, lo:hi], ACT.Identity, bias=bias[:, r:r + 1],
                                          scale=scale[:, r:r + 1])
                return last

            def stage_a(W, a, b, now, t):
                if now == W["GT"]:
                    act.wait_ge(s_gt, a.of(1, 1))
                    for o in range(2):
                        last = act.activation(pair(GTs)[0:KD, o], halves(A[0])[o * KD:(o + 1) * KD], ACT.Copy)
                    last.then_inc(s_gth, 1)
                if now == W["E"]:
                    for c in range(2):
                        act.wait_ge(s_e, a.of(2, c + 1))
                        for r in range(2):
                            last = act.activation(Fw[a.par][:, 2 * c + r, :], A[1 - c][:, r * D:(r + 1) * D], ACT.Square,
                                                  accum_out=ss[:, 2 * c + r:2 * c + r + 1])
                        last.then_inc(s_sq, 1)
                if now == W["XN"]:
                    act.wait_ge(s_ps, a.of(8, 8))
                    if not (isinstance(a.n, int) and a.n == 0):
                        act.wait_ge(s_zt, a.of(2, 0))
                    normed(Fw[a.par], sbias, sscl).then_inc(s_xna, 1)
                if now == W["XT"]:
                    act.wait_ge(s_xt, a.of(2, 1))
                    act.activation(X0h[:, :].rearrange("q (p r) -> q p r", r=TR),
                                   A[1][:, :].rearrange("q (r p) -> q p r", r=TR), ACT.Copy).then_inc(s_xh, 1)
                    act.wait_ge(s_xt, a.of(2, 2))
                    for o in range(2):
                        last = act.activation(pair_tok(X1)[0:DR, o], halves(A[0])[o * DR:(o + 1) * DR], ACT.Copy)
                    last.then_inc(s_xh, 1)
                if now == W["QK"][0]:
                    act.wait_ge(s_qk, a.of(3, 1))
                    act.activation(Q0h[:, :], A[1][:, :], ACT.Identity, bias=bqk[:, 0:1]).then_inc(s_qkh, 1)
                if now == W["QK"][1]:
                    act.wait_ge(s_qk, a.of(3, 2))
                    act.activation(K0h[:, :], A[0][:, :], ACT.Identity, bias=bqk[:, 1:2]).then_inc(s_qkh, 1)
                if now == W["QK"][2]:
                    act.wait_ge(s_qk, a.of(3, 3))
                    act.activation(K1h[0:KD, :], A[1][KD:P, :], ACT.Identity, bias=bqk[KD:P, 2:3])
                    act.activation(K1h[KD:P, :], A[1][KD:P, :], ACT.Identity, bias=bqk[KD:P, 2:3])
                    act.activation(Q1[0:KD, :], A[1][0:KD, :], ACT.Identity, bias=bqk[0:KD, 2:3])\
                       .then_inc(s_qkh, 1)
                for c in range(2):
                    if now == W["V"][c]:
                        act.wait_ge(s_v, a.of(2, c + 1))
                        act.activation(Vh[:, 2 * c:2 * c + 2, :], two(A[c]), ACT.Copy).then_inc(s_vh, 1)
                    if now == W["EXP"][c]:
                        act.wait_ge(s_nb, a.of(2, c + 1))
                        for q in range(QT):
                            last = act.activation(Pr[:, c, q, :], B[c][:, q * SEQ:(q + 1) * SEQ], ACT.Exp,
                                                  bias=nb[:, c, q:q + 1], scale=SCALE,
                                                  accum_out=rs[:, c, q:q + 1])
                        last.then_inc(s_ex, 1)
                    if now == W["PT"][c]:
                        act.wait_ge(s_pt, a.of(2, c + 1))
                        act.activation(PTh[:, c, :, :], B[c][:, :].rearrange("p (t q) -> p t q", t=QT), ACT.Copy)\
                           .then_inc(s_pth, 1)

            def stage_b(W, b, now):
                for c in range(2):
                    if now == W["Y"][c]:
                        act.wait_ge(s_y, b.of(2, c + 1))
                        act.wait_ge(s_ri, b.of(2, c + 1))
                        for q in range(QT):
                            last = act.activation(Yh[:, q, :, c, :],
                                                  two(B[c])[:, q, :].rearrange("p (a c) -> p c a", c=3),
                                                  ACT.Identity, scale=ri[:, c, q:q + 1])
                        last.then_inc(s_yh, 1)
                if now == W["XN2"]:
                    act.wait_ge(s_p2, b.of(3, 3))
                    normed(h2[b.par], s2bias, s2).then_inc(s_xn2a, 1)
                if now == W["ZT"]:
                    act.wait_ge(s_zt, b.of(2, 1))
                    act.activation(Z0h[b.par][:, :], B[0][:, :], ACT.Copy).then_inc(s_zh, 1)
                    act.wait_ge(s_zt, b.of(2, 2))
                    for o in range(2):
                        last = act.activation(pair(Z1[b.par])[0:DR, o], halves(B[1])[o * DR:(o + 1) * DR], ACT.Copy)
                    last.then_inc(s_zh, 1)
                if now == W["RT"]:
                    act.wait_ge(s_lg, b.of(1, 1))
                    act.activation(rt[:, 0, :, :], rt[:, 13, :, :], ACT.Exp, scale=-1.0).then_inc(s_re, 1)
                if now == W["CT"]:
                    act.wait_ge(s_ct, b.of(1, 1))
                    if not (isinstance(b.n, int) and b.n == 0):
                        act.wait_ge(s_cd, b.of(16, 0))
                    act.activation(combT[P - TR * NE:P, :], B[1][P - TR * NE:P, 0:P], ACT.Copy).then_inc(s_cs, 1)

            def step(a, b, m, t):
                W = table(a, b, m)["act"]
                for now in range(NCH * TICKS):
                    k = now // TICKS
                    j, g = chunk_at(k, 1, m, t)
                    if a is not None and m is None and now % TICKS == 0:
                        split(k if b is None else k + NCH)
                    if now % TICKS == W["SQUARE"]:
                        if g is not None:
                            if j < ECH:
                                act.wait_ge(s_t, g.of(ECH, j + 1))
                                act.activation(U[j % 2][:, :], U[j % 2][:, :], ACT.Square).then_inc(s_u, 1)
                            else:
                                act.wait_ge(s_r, g.of(NCH, j + 1))
                                act.wait_ge(s_ul, g.of(NCH, j - 1))
                                act.activation(U[j % 2][:, :], R[j % 2][:, :], ACT.Square).then_inc(s_u, 1)
                    if now % TICKS == W["RELU"]:
                        if m is not None:
                            act.wait_ge(s_up, m.of(NCH, k + 1))
                            if t is not None or k >= 2:
                                act.wait_ge(s_u, m.of(NCH, k - 1))
                            act.activation(R[k % 2][:, :], UB[k % 2][:, :], ACT.Relu).then_inc(s_r, 1)
                    if now % TICKS == W["HI"]:
                        if g is not None:
                            act.wait_ge(s_u, g.of(NCH, j + 1))
                            if j >= NU:
                                act.wait_ge(s_dn, g.of(NCH, j - NU + 1))
                            elif not (isinstance(g.n, int) and g.n == 0):
                                act.wait_ge(s_dn, g.of(NCH, (-1, 0, -2)[j]))
                            act.activation(Uh[j % NU][:, :], U[j % 2][:, :], ACT.Copy).then_inc(s_uh, 1)
                    if t is not None and now == W["ACC"]:
                        act.wait_ge(s_dn, t.of(NCH, NCH))
                        for c in range(2):
                            act.activation(ACS[t.par][c], AC[c][:, :], ACT.Copy).then_inc(s_acc, 1)
                    if a is not None:
                        stage_a(W, a, b, now, t)
                    if b is not None:
                        stage_b(W, b, now)

            schedule(act, step)

        @block.vector
        def _(dve):
            dve.memset(ones[:, :].bitcast(f32), 1.0).then_inc(s_ones, 1)
            dve.memset(K1l[KD:P, :].bitcast(f32), 0.0).then_inc(s_ones, 1)
            dve.wait_ge(s_ids, 16)
            dve.tensor_copy(idf[:, :, :], ids[:, :, :]).then_inc(s_rows, 1)
            dve.wait_ge(s_rows, 1)
            dve.tensor_scalar(neg[:, :, :], idf[:, :, :], 0.0, float(VOCAB), ALU.is_lt, ALU.mult).then_inc(s_rows, 1)
            dve.wait_ge(s_rows, 2)
            dve.tensor_tensor(neg[:, :, :], idf[:, :, :], neg[:, :, :], ALU.add).then_inc(s_rows, 1)
            dve.wait_ge(s_rows, 3)
            dve.tensor_scalar(idf[:, :, :], neg[:, :, :], 0.0, float(VOCAB - 1), ALU.max, ALU.min).then_inc(s_rows, 1)
            dve.wait_ge(s_rows, 4)
            dve.tensor_copy(rows[:, :, :], idf[:, :, :]).then_inc(s_rows, 1)

            def lows(made, pieces):
                for n, (src, hi, lo) in enumerate(pieces):
                    dve.wait_ge(s_whi, made + n + 1)
                    dve.tensor_tensor(lo, src, hi.bitcast(f32), ALU.subtract).then_inc(s_wlo, 1)

            lows(0, proj_w)

            def split(k):
                if k == QK_SLOT:
                    lows(N_PROJ, qk_w)
                if k == REST_SLOT:
                    lows(N_QK, rest_w)
                    dve.wait_ge(s_whi, N_REST)
                    dve.tensor_tensor(BVC[32:33, :], rB[32:33, :], BVC[32:33, :].bitcast(f32), ALU.subtract).then_inc(s_wlo, 1)
                for n, piece in mlp_split_at(k):
                    lows(n, [piece])

            def stage_a(W, a, now):
                if now == W["GT"]:
                    dve.wait_ge(s_gth, a.of(1, 1))
                    for o in range(2):
                        last = dve.tensor_tensor(pair(GTs)[KD:P, o], halves(A[0])[o * KD:(o + 1) * KD],
                                                 pair(GTs)[0:KD, o].bitcast(f32), ALU.subtract)
                    last.then_inc(s_gtl, 1)
                if now == W["E"]:
                    for c in range(2):
                        dve.wait_ge(s_sq, a.of(2, c + 1))
                        dve.tensor_tensor(Fw[a.par][:, 2 * c:2 * c + 2, :], two(A[1 - c]),
                                          normw[:, :].unsqueeze(1).to_broadcast([P, 2, D]), ALU.mult).then_inc(s_fw, 1)
                if now == W["XT"]:
                    dve.wait_ge(s_xh, a.of(2, 1))
                    dve.tensor_tensor(X0l[:, :].rearrange("q (p r) -> q p r", r=TR),
                                      A[1][:, :].rearrange("q (r p) -> q p r", r=TR),
                                      X0h[:, :].bitcast(f32).rearrange("q (p r) -> q p r", r=TR),
                                      ALU.subtract).then_inc(s_xl, 1)
                    dve.wait_ge(s_xh, a.of(2, 2))
                    for o in range(2):
                        last = dve.tensor_tensor(pair_tok(X1)[DR:P, o], halves(A[0])[o * DR:(o + 1) * DR],
                                                 pair_tok(X1)[0:DR, o].bitcast(f32), ALU.subtract)
                    last.then_inc(s_xl, 1)
                if now == W["QK"][0]:
                    dve.wait_ge(s_qkh, a.of(3, 1))
                    dve.scalar_tensor_tensor(Q0l[:, :], A[1][:, :], bqk[:, 0:1], Q0h[:, :].bitcast(f32),
                                             ALU.add, ALU.subtract).then_inc(s_qkl, 1)
                if now == W["QK"][1]:
                    dve.wait_ge(s_qkh, a.of(3, 2))
                    dve.scalar_tensor_tensor(K0l[:, :], A[0][:, :], bqk[:, 1:2], K0h[:, :].bitcast(f32),
                                             ALU.add, ALU.subtract).then_inc(s_qkl, 1)
                if now == W["QK"][2]:
                    dve.wait_ge(s_qkh, a.of(3, 3))
                    dve.scalar_tensor_tensor(K1l[0:KD, :], A[1][KD:P, :], bqk[KD:P, 2:3],
                                             K1h[KD:P, :].bitcast(f32), ALU.add, ALU.subtract)
                    dve.scalar_tensor_tensor(Q1[KD:P, :], A[1][0:KD, :], bqk[0:KD, 2:3],
                                             Q1[0:KD, :].bitcast(f32), ALU.add, ALU.subtract).then_inc(s_qkl, 1)
                for c in range(2):
                    if now == W["V"][c]:
                        dve.wait_ge(s_vh, a.of(2, c + 1))
                        dve.tensor_tensor(Vl[:, 2 * c:2 * c + 2, :], two(A[c]),
                                          Vh[:, 2 * c:2 * c + 2, :].bitcast(f32), ALU.subtract).then_inc(s_vl, 1)
                    if now == W["PT"][c]:
                        dve.wait_ge(s_pth, a.of(2, c + 1))
                        dve.tensor_tensor(PTl[:, c, :, :], B[c][:, :].rearrange("p (t q) -> p t q", t=QT),
                                          PTh[:, c, :, :].bitcast(f32), ALU.subtract).then_inc(s_ptl, 1)
                if now == W["BN"]:
                    dve.wait_ge(s_fw, a.of(2, 2))
                    for r in range(TR):
                        last = dve.bn_stats(st[:, r, :], Fw[a.par][:, r, :])
                    last.then_inc(s_st, 1)
                    moments(a, st, mm, s_st, s_mv)
                if now == W["XN"]:
                    dve.wait_ge(s_ps, a.of(8, 8))
                    if not (isinstance(a.n, int) and a.n == 0):
                        dve.wait_ge(s_zt, a.of(2, 0))
                    normed(Fw[a.par], mm[:, 3, :], sscl).then_inc(s_xn, 1)
                for c in range(2):
                    if now == W["S"][c]:
                        dve.wait_ge(s_s, a.of(2, c + 1))
                        dve.tensor_reduce(mx[:, c, :], B[c][:, :].rearrange("p (q s) -> p q s", q=QT), AX.X, ALU.max)\
                           .then_inc(s_mx, 1)
                        dve.wait_ge(s_mx, a.of(2, c + 1))
                        dve.tensor_scalar(nb[:, c, :], mx[:, c, :], -SCALE, None, ALU.mult).then_inc(s_nb, 1)
                    if now == W["EXP"][c]:
                        dve.wait_ge(s_ex, a.of(2, c + 1))
                        dve.reciprocal(ri[:, c, :], rs[:, c, :]).then_inc(s_ri, 1)

            def stage_b(W, b, now, t):
                for c in range(2):
                    if now == W["Y"][c]:
                        dve.wait_ge(s_yh, b.of(2, c + 1))
                        for q in range(QT):
                            last = dve.scalar_tensor_tensor(Yl[:, q, :, c, :],
                                                            two(B[c])[:, q, :].rearrange("p (a c) -> p c a", c=3),
                                                            ri[:, c, q:q + 1], Yh[:, q, :, c, :].bitcast(f32),
                                                            ALU.mult, ALU.subtract)
                        last.then_inc(s_yl, 1)
                if now == W["WC"]:
                    if t is not None:
                        dve.wait_ge(s_res, t.of(1, 1))
                    for c in range(2):
                        dve.wait_ge(s_wc, b.of(2, c + 1))
                        for r in (2 * c, 2 * c + 1):
                            last = dve.scalar_tensor_tensor(h2[b.par][:, r, :], Fw[b.par][:, r, :], sr1[b.par][:, r:r + 1],
                                                            two(B[c])[:, r % 2, :], ALU.mult, ALU.add)
                        last.then_inc(s_h2, 1)
                        dve.wait_ge(s_h2, b.of(2, c + 1))
                        for r in (2 * c, 2 * c + 1):
                            last = dve.bn_stats(st2[:, r, :], h2[b.par][:, r, :])
                    last.then_inc(s_st2, 1)
                    moments(b, st2, mm2, s_st2, s_mv2)
                if now == W["RT"]:
                    dve.wait_ge(s_rt, b.of(1, 1))
                    dve.tensor_reduce(rt[:, 13, :, :], B[0][:, 0:2 * TR * NE].rearrange("p (r a e) -> p r e a", r=TR, a=2),
                                      AX.X, ALU.add).then_inc(s_lg, 1)
                if now == W["ZT"]:
                    dve.wait_ge(s_zh, b.of(2, 1))
                    dve.tensor_tensor(Z0l[b.par][:, :], B[0][:, :], Z0h[b.par][:, :].bitcast(f32), ALU.subtract)\
                       .then_inc(s_zl, 1)
                    dve.wait_ge(s_zh, b.of(2, 2))
                    for o in range(2):
                        last = dve.tensor_tensor(pair(Z1[b.par])[DR:P, o], halves(B[1])[o * DR:(o + 1) * DR],
                                                 pair(Z1[b.par])[0:DR, o].bitcast(f32), ALU.subtract)
                    last.then_inc(s_zl, 1)
                if now == W["XN2"]:
                    dve.wait_ge(s_p2, b.of(3, 3))
                    normed(h2[b.par], mm2[:, 3, :], s2).then_inc(s_xn2, 1)
                if now in W["ROUTE"]:
                    route(b, W["ROUTE"].index(now))

            def step(a, b, m, t):
                W = table(a, b, m)["dve"]
                for now in range(NCH * TICKS):
                    k = now // TICKS
                    if a is not None and m is None and now % TICKS == 0:
                        split(k if b is None else k + NCH)
                    if now % TICKS == W["LO"]:
                        j, g = chunk_at(k, 1, m, t)
                        if g is not None:
                            dve.wait_ge(s_uh, g.of(NCH, j + 1))
                            half, to = (slice(0, P), Ul) if j < NCH - 1 else (slice(KD, P), Uh)
                            dve.tensor_tensor(to[j % NU][half, :], U[j % 2][half, :],
                                              Uh[j % NU][half, :].bitcast(f32), ALU.subtract)\
                               .then_inc(s_ul, 1)
                    if t is not None and now == W["OUT"]:
                        dve.wait_ge(s_res, t.of(1, 1))
                        for c in range(2):
                            dve.wait_ge(s_op, t.of(2, c + 1))
                            res = OUT[t.par][:, 2 * c * D:(2 * c + 2) * D].rearrange("p (r d) -> p r d", r=2)
                            dve.tensor_tensor(res, two(A[c]), res, ALU.add).then_inc(s_ot, 1)
                    if a is not None:
                        stage_a(W, a, now)
                    if b is not None:
                        stage_b(W, b, now, t)

            def normed(src, less_mean, scale):
                for r, lo, hi, at in XN_PARTS[0]:
                    last = dve.tensor_scalar(xn[:, 0, at:at + hi - lo], src[:, r, lo:hi], less_mean[:, r:r + 1],
                                             scale[:, r:r + 1], ALU.add, ALU.mult)
                return last

            def moments(g, stats, to, s_in, s_to):
                dve.wait_ge(s_in, g.of(1, 1))
                dve.tensor_tensor(to[:, 0, :], stats[:, :, 1], stats[:, :, 4], ALU.add)
                dve.tensor_tensor(to[:, 1, :], stats[:, :, 1], stats[:, :, 4], ALU.subtract)
                dve.tensor_tensor(to[:, 2, :], stats[:, :, 2], stats[:, :, 5], ALU.add).then_inc(s_to, 1)
                dve.wait_ge(s_to, g.of(3, 1))
                dve.tensor_scalar(to[:, 3, :], to[:, 0, :], -0.5, None, ALU.mult)
                dve.tensor_tensor(to[:, 4, :], to[:, 1, :], to[:, 1, :], ALU.mult).then_inc(s_to, 1)
                dve.wait_ge(s_to, g.of(3, 2))
                dve.scalar_tensor_tensor(to[:, 5, :], to[:, 4, :], D / 4.0, to[:, 2, :], ALU.mult, ALU.add).then_inc(s_to, 1)

            def route(b, part):
                c = (0, 6, 12)[part]

                def link(ins):
                    nonlocal c
                    c += 1
                    ins.then_inc(s_rc, 1)
                    dve.wait_ge(s_rc, b.of(NRC, c))

                def wide(i):
                    return rm[:, i, :].unsqueeze(2).to_broadcast([P, TR, NE])

                def largest(one, sel):
                    link(dve.tensor_reduce(rm[:, 2 * one, :], rt[:, sel, :, :], AX.X, ALU.max))
                    link(dve.tensor_tensor(rt[:, 4 + 4 * one, :, :], rt[:, sel, :, :], wide(2 * one), ALU.is_equal))

                if part == 0:
                    dve.wait_ge(s_re, b.of(1, 1))
                    link(dve.tensor_scalar(rt[:, 1, :, :], rt[:, 0, :, :], 1.0, None, ALU.add))
                    link(dve.reciprocal(rt[:, 2, :, :], rt[:, 1, :, :]))
                    link(dve.tensor_tensor(rt[:, 3, :, :], rt[:, 2, :, :],
                                           balb[:, :].unsqueeze(1).to_broadcast([P, TR, NE]), ALU.add))
                    largest(0, 3)
                    link(dve.tensor_tensor(rt[:, 5, :, :], rt[:, 4, :, :], rank[:, :, :], ALU.mult))
                    assert c == 6, c
                if part == 1:
                    link(dve.tensor_reduce(rm[:, 1, :], rt[:, 5, :, :], AX.X, ALU.max))
                    link(dve.tensor_tensor(rt[:, 6, :, :], rt[:, 5, :, :], wide(1), ALU.is_equal))
                    link(dve.scalar_tensor_tensor(rt[:, 7, :, :], rt[:, 6, :, :], -BIG, rt[:, 3, :, :], ALU.mult, ALU.add))
                    largest(1, 7)
                    link(dve.tensor_tensor(rt[:, 9, :, :], rt[:, 8, :, :], rank[:, :, :], ALU.mult))
                    assert c == 12, c
                if part == 2:
                    link(dve.tensor_reduce(rm[:, 3, :], rt[:, 9, :, :], AX.X, ALU.max))
                    link(dve.tensor_tensor(rt[:, 10, :, :], rt[:, 9, :, :], wide(3), ALU.is_equal))
                    link(dve.tensor_tensor(rt[:, 11:13, :, :], rt[:, 6:11:4, :, :],
                                           rt[:, 2, :, :].unsqueeze(1).to_broadcast([P, 2, TR, NE]), ALU.mult))
                    link(dve.tensor_reduce(rm[:, 4:6, :], rt[:, 11:13, :, :], AX.X, ALU.add))
                    link(dve.scalar_tensor_tensor(rm[:, 6, :], rm[:, 4, :], EPS_TOP, rm[:, 5, :], ALU.add, ALU.add))
                    link(dve.reciprocal(rm[:, 7, :], rm[:, 6, :]))
                    dve.tensor_tensor(rm[:, 8:10, :], rm[:, 4:6, :],
                                      rm[:, 7, :].unsqueeze(1).to_broadcast([P, 2, TR]), ALU.mult).then_inc(s_comb, 1)
                    assert c == NRC, c

            schedule(dve, step)

        @block.tensor
        def _(pe):
            pe.wait_ge(s_const, 15)
            pe.wait_ge(s_ones, 2)

            def split5(dst, s0h, s0l, s1, mvh, mvl, m1h, m1l, start):
                pe.matmul(dst, s0h, mvh, start=start, stop=False, skip_group_check=True)
                pe.matmul(dst, s0h, mvl, start=False, stop=False, skip_group_check=True)
                pe.matmul(dst, s0l, mvh, start=False, stop=False, skip_group_check=True)
                pe.matmul(dst, s1, m1h, start=False, stop=False, skip_group_check=True)
                return pe.matmul(dst, s1, m1l, start=False, stop=True, skip_group_check=True)

            def bias2(bank, cols):
                pe.matmul(two(bank), ones[:, :], BVC[:, cols].unsqueeze(1).to_broadcast([P, 2, D]), start=True, stop=False,
                          skip_group_check=True)

            def weights5(dst, w0h, w0l, w1h, w1l, xh, xl, x1):
                pe.matmul(dst, w0h, xh, start=True, stop=False)
                pe.matmul(dst, w0h, xl, start=False, stop=False)
                pe.matmul(dst, w0l, xh, start=False, stop=False)
                pe.matmul(dst, w1h, x1, start=False, stop=False)
                return pe.matmul(dst, w1l, x1, start=False, stop=True)

            def stage_a(W, a, now, t):
                later = not (isinstance(a.n, int) and a.n == 0)
                if now == W["GT"]:
                    pe.wait_ge(s_gath[a.par], a.half * 64 + 64)
                    if later:
                        pe.wait_ge(s_vl, a.of(2, -1))
                    for c in range(2):
                        last = pe.transpose(A[0][:, c * P:(c + 1) * P],
                                            G[a.par][:, 2 * c:2 * c + 2, :].rearrange("p r k -> p (r k)"), ident[:, :])
                    last.then_inc(s_gt, 1)
                if now == W["E"]:
                    if not later:
                        pe.wait_ge(s_wlo, N_PROJ)
                    else:
                        pe.wait_ge(s_vl, a.of(2, 0))
                    pe.wait_ge(s_gtl, a.of(1, 1))
                    for c in range(2):
                        for r in range(2):
                            dst = two(A[1 - c])[:, r, :]
                            lhs = GTs[:, (2 * c + r) * P:(2 * c + r + 1) * P]
                            pe.matmul(dst, lhs, PJh[:, :], start=True, stop=False)
                            last = pe.matmul(dst, lhs, PJl[:, :], start=False, stop=True)
                        last.then_inc(s_e, 1)
                if now == W["XT"]:
                    pe.wait_ge(s_xn, a.of(1, 1))
                    pe.wait_ge(s_xna, a.of(1, 1))
                    if t is not None:
                        pe.wait_ge(s_ot, t.of(2, 2))
                    for r in range(TR):
                        last = pe.transpose(A[1][:, r * P:(r + 1) * P], xn[:, r // 2, r % 2 * 2 * P:r % 2 * 2 * P + P], ident[:, :])
                    last.then_inc(s_xt, 1)
                    for c in range(2):
                        last = pe.transpose(A[0][:, c * P:(c + 1) * P], xn[:, c, P:2 * P], ident[:, :])
                    last.then_inc(s_xt, 1)
                if now in W["QK"]:
                    c = W["QK"].index(now)
                    if c == 0:
                        if not later:
                            pe.wait_ge(s_wlo, N_QK)
                        pe.wait_ge(s_xl, a.of(2, 2))
                    if c == 2:
                        pe.wait_ge(s_qkl, a.of(3, 1))
                    cols = slice(c * P, (c + 1) * P)
                    weights5(A[(1 + c) % 2][:, :], QK0h[:, cols], QK0l[:, cols], QK1h[:, cols], QK1l[:, cols],
                             X0h[:, :], X0l[:, :], X1[:, :]).then_inc(s_qk, 1)
                if now in W["V"]:
                    c = W["V"].index(now)
                    if c == 0 and not later:
                        pe.wait_ge(s_wlo, N_REST)
                    pe.wait_ge(s_qkl, a.of(3, 2 + c))
                    bias2(A[c], slice(0, D))
                    for r in range(2):
                        tok = slice((2 * c + r) * P, (2 * c + r + 1) * P)
                        last = split5(two(A[c])[:, r, :], X0h[:, tok], X0l[:, tok], X1[:, tok], WV0h[:, :], WV0l[:, :],
                                      WV1h[:, :], WV1l[:, :], False)
                    last.then_inc(s_v, 1)
                if now in W["S"]:
                    c = W["S"].index(now)
                    pe.wait_ge(s_qkl, a.of(3, 3))
                    if later:
                        pe.wait_ge(s_lg if c == 0 else s_cs, a.of(1, 0))
                    for q in range(QT):
                        qs = slice(c * SEQ + q * P, c * SEQ + (q + 1) * P)
                        ks = slice(c * SEQ, (c + 1) * SEQ)
                        last = split5(B[c][:, q * SEQ:(q + 1) * SEQ], Q0h[:, qs], Q0l[:, qs], Q1[:, qs], K0h[:, ks],
                                      K0l[:, ks], K1h[:, ks], K1l[:, ks], True)
                    last.then_inc(s_s, 1)

                if now in W["PT"]:
                    c = W["PT"].index(now)
                    pe.wait_ge(s_ex, a.of(2, c + 1))
                    for q in range(QT):
                        for kt in range(QT):
                            last = pe.transpose(B[c][:, kt * SEQ + q * P:kt * SEQ + (q + 1) * P],
                                                Pr[:, c, q, kt * P:(kt + 1) * P], ident[:, :])
                    last.then_inc(s_pt, 1)

            WC_UNITS = [[(0, 0, 0), (1, 0, 2)], [(1, 0, 3), (0, 1, 1)], [(1, 1, 0), (0, 2, 2)], [(0, 2, 3), (1, 2, 1)]]

            def stage_b(W, b, now):
                if now in W["Y"]:
                    c = W["Y"].index(now)
                    pe.wait_ge(s_ptl, b.of(2, c + 1))
                    pe.wait_ge(s_vl, b.of(2, 2))
                    for q in range(QT):
                        dst = two(B[c])[:, q, :]
                        for kt in range(QT):
                            qs, v = slice(q * P, (q + 1) * P), c * QT + kt
                            pe.matmul(dst, PTh[:, c, kt, qs], Vh[:, v, :], start=kt == 0, stop=False, skip_group_check=True)
                            pe.matmul(dst, PTh[:, c, kt, qs], Vl[:, v, :], start=False, stop=False, skip_group_check=True)
                            last = pe.matmul(dst, PTl[:, c, kt, qs], Vh[:, v, :], start=False, stop=kt == QT - 1,
                                             skip_group_check=True)
                    last.then_inc(s_y, 1)
                if now == W["WC"]:
                    pe.wait_ge(s_yl, b.of(2, 2))
                    for c in range(2):
                        bias2(B[c], slice(D, 2 * D))
                        for r in range(2):
                            dst = two(B[c])[:, r, :]
                            for n, (qt, e3, w) in enumerate(WC_UNITS[2 * c + r]):
                                yh = Yh[:, qt, e3, :, :].rearrange("p s a -> p (s a)")
                                yl = Yl[:, qt, e3, :, :].rearrange("p s a -> p (s a)")
                                pe.matmul(dst, yh, WCh[:, w, :], start=False, stop=False, skip_group_check=True)
                                pe.matmul(dst, yh, WCl[:, w, :], start=False, stop=False, skip_group_check=True)
                                last = pe.matmul(dst, yl, WCh[:, w, :], start=False, stop=n == 1, skip_group_check=True)
                        last.then_inc(s_wc, 1)
                if now == W["ZT"]:
                    pe.wait_ge(s_xn2, b.of(1, 1))
                    pe.wait_ge(s_xn2a, b.of(1, 1))
                    for r in range(TR):
                        last = pe.transpose(B[0][:, r * P:(r + 1) * P], xn[:, r // 2, r % 2 * 2 * P:r % 2 * 2 * P + P], ident[:, :])
                    last.then_inc(s_zt, 1)
                    for c in range(2):
                        last = pe.transpose(B[1][:, c * P:(c + 1) * P], xn[:, c, P:2 * P], ident[:, :])
                    last.then_inc(s_zt, 1)
                if now == W["RT"]:
                    pe.wait_ge(s_zl, b.of(2, 2))
                    z0h, z0l, z1 = Z0h[b.par], Z0l[b.par], Z1[b.par]
                    for r in range(TR):
                        tok = slice(r * P, (r + 1) * P)
                        dst = B[0][:, 2 * r * NE:2 * (r + 1) * NE]
                        w0, w1 = [w[:, :, :].rearrange("p a e -> p (a e)") for w in (RW0, RW1)]
                        pe.matmul(dst, z0h[:, tok], w0, start=True, stop=False, skip_group_check=True)
                        pe.matmul(dst, z0l[:, tok], w0, start=False, stop=False, skip_group_check=True)
                        last = pe.matmul(dst, z1[:, tok], w1, start=False, stop=True, skip_group_check=True)
                    last.then_inc(s_rt, 1)
                if now == W["CT"]:
                    pe.wait_ge(s_root, b.of(3, 3))
                    pe.transpose(B[1][:, 0:P], rt[:, 10:14, :, :].rearrange("p i r e -> p (i r e)"), ident[:, :])\
                      .then_inc(s_ct, 1)

            def step(a, b, m, t):
                W = table(a, b, m)["pe"]
                for now in range(NCH * TICKS):
                    k = now // TICKS
                    if now % TICKS == W["UP"]:
                        if m is not None:
                            if k == 0:
                                pe.wait_ge(s_zl, m.of(2, 2))
                                if t is None:
                                    pe.wait_ge(s_wlo, N_ALL)
                            if t is not None or k >= 2:
                                pe.wait_ge(s_r, m.of(NCH, k - 1))
                            cols = slice(k * P, (k + 1) * P)
                            weights5(UB[k % 2][:, :], UP0h[:, cols], UP0l[:, cols], UP1h[:, cols], UP1l[:, cols],
                                     Z0h[m.par][:, :], Z0l[m.par][:, :], Z1[m.par][:, :]).then_inc(s_up, 1)
                    if now % TICKS == W["DOWN"]:
                        for j, g in downs_at(k, m, t):
                            pe.wait_ge(s_ul, g.of(NCH, j + 1))
                            if j == 0 and t is not None:
                                pe.wait_ge(s_acc, g.of(2, 0))
                            uh, ul = Uh[j % NU][:, :], Ul[j % NU][:, :]
                            w0h, w0l, w1 = DN0h[:, j, :], DN0l[:, j, :], DN1[:, j, :]
                            whole = j < NCH - 1
                            pe.matmul(AC[0][:, :], w0h, uh, start=j == 0, stop=False)
                            pe.matmul(AC[0][:, :], w0l, uh, start=False, stop=not whole)
                            if whole:
                                pe.matmul(AC[0][:, :], w0h, ul, start=False, stop=False)
                            last = pe.matmul(AC[1][:, :], w1, uh, start=j == 0, stop=not whole)
                            if whole:
                                last = pe.matmul(AC[1][:, :], w1, ul, start=False, stop=False)
                            last.then_inc(s_dn, 1)
                    if t is not None and now == W["OUT"]:
                        pe.wait_ge(s_acc, t.of(2, 2))
                        if a is not None:
                            pe.wait_ge(s_fw, a.of(2, 2))
                        elif not (isinstance(t.n, int) and t.n == 0):
                            pe.wait_ge(s_ot, t.of(2, 0))
                        for c in range(TR):
                            dst = two(A[c // 2])[:, c % 2, :]
                            tok = slice(c * P, (c + 1) * P)
                            pe.transpose(dst[:, 0:P], ACS[t.par][0][:, tok], ident[:, :])
                            last = pe.matmul(dst[:, P:D], ACS[t.par][1][:, tok], fold[:, :], start=True, stop=True,
                                             skip_group_check=True)
                            if c % 2:
                                last.then_inc(s_op, 1)
                    if b is not None:
                        stage_b(W, b, now)
                    if a is not None:
                        stage_a(W, a, now, t)

            schedule(pe, step)


_IN = ["x", "coords", "w_proj", "norm_w", "w_qk", "b_qk", "w_v", "b_v", "w_c", "b_c", "w_up", "w_down", "w_router", "b_bal"]


def kernel(**inputs):
    import numpy as np
    import concourse.bacc as bacc
    from concourse.bass_utils import run_bass_kernel_spmd

    a = {k.replace("L0_", ""): np.asarray(v) for k, v in inputs.items()}
    wq, wk = a["attn_Wq"].T, a["attn_Wk"].T
    bq, bk = a["attn_bq"], a["attn_bk"]
    up = np.concatenate([a["ffn_w1"].transpose(1, 0, 2).reshape(D, NE * D), a["ffn_w_fc_sh"]], axis=1)
    down = np.concatenate([a["ffn_w2"].reshape(NE * D, D), a["ffn_w_proj_sh"]], axis=0)
    laid = {
        "x": a["x"], "coords": a["tok_basin_coords"], "w_proj": a["tok_proj_w"].T, "norm_w": a["tok_norm_w"],
        "w_qk": np.concatenate([wq[:, :P], wk[:, :P], wq[:, P:], wk[:, P:]], axis=1),
        "b_qk": np.concatenate([bq[:P], bk[:P], bq[P:], bk[P:]]).reshape(3, P).T,
        "w_v": a["attn_Wv"].T, "b_v": a["attn_bv"], "w_c": a["attn_Wc"].T, "b_c": a["attn_bc"],
        "w_up": np.concatenate([up, up[:, HID - (HP - HID):]], axis=1),
        "w_down": np.concatenate([down, down[HID - (HP - HID):]], axis=0),
        "w_router": a["ffn_router_w"].T, "b_bal": a["ffn_balance_bias"],
    }
    nc = bacc.Bacc("TRN2", target_bir_lowering=False, num_devices=1)
    arrays, args = {}, []
    for name in _IN:
        v = np.ascontiguousarray(laid[name])
        arrays[f"in_{name}"] = v
        args.append(nc.dram_tensor(f"in_{name}", v.shape, mybir.dt.from_np(v.dtype), kind="ExternalInput").ap())
    args.append(nc.dram_tensor("out_y", (BATCH, SEQ, D), mybir.dt.float32, kind="ExternalOutput").ap())
    tower_kernel(nc, *args)
    r = run_bass_kernel_spmd(nc, [arrays], core_ids=[0])
    return r.results[0]["out_y"]
```
